# Optimizing a Trainium2 kernel written in Bass

```python
import numpy as np
import jax
import jax.numpy as jnp

def _softmax(x, axis=-1):
    return jax.nn.softmax(x, axis=axis)

def _gelu(x):
    return jax.nn.gelu(x, approximate=True)

def _silu(x):
    return jax.nn.silu(x)

def _sigmoid(x):
    return jax.nn.sigmoid(x)

def _layernorm(x, axis=-1, eps=1e-05):
    m = jnp.mean(x, axis=axis, keepdims=True)
    v = jnp.var(x, axis=axis, keepdims=True)
    return (x - m) / jnp.sqrt(v + eps)

def _scatter_add(tgt, idx, src, axis=0):
    return tgt.at[idx].add(src)

def _segment_sum(src, seg, n):
    return jax.ops.segment_sum(src, seg, n)
kernel_name = 'mk_dlrm_tower_d1_rec_r8_9e8cac'

def setup_inputs(seed: int=0):
    np.random.seed(seed)
    _w = jnp.asarray

    def _rec_inputs():
        import jax
        import jax.numpy as jnp
        _tk = jax.random.key(seed)
        dense_ctx = jax.random.normal(jax.random.fold_in(_tk, 190), (2048, 16), jnp.float32)
        ids = jnp.stack([jax.random.randint(jax.random.fold_in(_tk, 200 + f), (2048,), 0, v, jnp.int32) for f, v in enumerate([12500, 125000, 12500, 1250, 125000, 1250, 1000, 1250, 1000, 1250, 1000, 1000, 1000, 125000, 125000, 1000, 12500, 12500, 1250, 1000, 12500, 1000, 1000, 1000, 125000, 1000, 12500, 12500, 125000, 12500, 12500, 1000, 1250, 1000, 12500, 12500, 1000, 1000, 12500, 1000])], axis=1)
        tbl_0 = 0.05 * jax.random.normal(jax.random.fold_in(_tk, 500 + 0), (12500, 32), jnp.float32)
        tbl_1 = 0.05 * jax.random.normal(jax.random.fold_in(_tk, 500 + 1), (125000, 32), jnp.float32)
        tbl_2 = 0.05 * jax.random.normal(jax.random.fold_in(_tk, 500 + 2), (12500, 32), jnp.float32)
        tbl_3 = 0.05 * jax.random.normal(jax.random.fold_in(_tk, 500 + 3), (1250, 32), jnp.float32)
        tbl_4 = 0.05 * jax.random.normal(jax.random.fold_in(_tk, 500 + 4), (125000, 32), jnp.float32)
        tbl_5 = 0.05 * jax.random.normal(jax.random.fold_in(_tk, 500 + 5), (1250, 32), jnp.float32)
        tbl_6 = 0.05 * jax.random.normal(jax.random.fold_in(_tk, 500 + 6), (1000, 32), jnp.float32)
        tbl_7 = 0.05 * jax.random.normal(jax.random.fold_in(_tk, 500 + 7), (1250, 32), jnp.float32)
        tbl_8 = 0.05 * jax.random.normal(jax.random.fold_in(_tk, 500 + 8), (1000, 32), jnp.float32)
        tbl_9 = 0.05 * jax.random.normal(jax.random.fold_in(_tk, 500 + 9), (1250, 32), jnp.float32)
        tbl_10 = 0.05 * jax.random.normal(jax.random.fold_in(_tk, 500 + 10), (1000, 32), jnp.float32)
        tbl_11 = 0.05 * jax.random.normal(jax.random.fold_in(_tk, 500 + 11), (1000, 32), jnp.float32)
        tbl_12 = 0.05 * jax.random.normal(jax.random.fold_in(_tk, 500 + 12), (1000, 32), jnp.float32)
        tbl_13 = 0.05 * jax.random.normal(jax.random.fold_in(_tk, 500 + 13), (125000, 32), jnp.float32)
        tbl_14 = 0.05 * jax.random.normal(jax.random.fold_in(_tk, 500 + 14), (125000, 32), jnp.float32)
        tbl_15 = 0.05 * jax.random.normal(jax.random.fold_in(_tk, 500 + 15), (1000, 32), jnp.float32)
        tbl_16 = 0.05 * jax.random.normal(jax.random.fold_in(_tk, 500 + 16), (12500, 32), jnp.float32)
        tbl_17 = 0.05 * jax.random.normal(jax.random.fold_in(_tk, 500 + 17), (12500, 32), jnp.float32)
        tbl_18 = 0.05 * jax.random.normal(jax.random.fold_in(_tk, 500 + 18), (1250, 32), jnp.float32)
        tbl_19 = 0.05 * jax.random.normal(jax.random.fold_in(_tk, 500 + 19), (1000, 32), jnp.float32)
        tbl_20 = 0.05 * jax.random.normal(jax.random.fold_in(_tk, 500 + 20), (12500, 32), jnp.float32)
        tbl_21 = 0.05 * jax.random.normal(jax.random.fold_in(_tk, 500 + 21), (1000, 32), jnp.float32)
        tbl_22 = 0.05 * jax.random.normal(jax.random.fold_in(_tk, 500 + 22), (1000, 32), jnp.float32)
        tbl_23 = 0.05 * jax.random.normal(jax.random.fold_in(_tk, 500 + 23), (1000, 32), jnp.float32)
        tbl_24 = 0.05 * jax.random.normal(jax.random.fold_in(_tk, 500 + 24), (125000, 32), jnp.float32)
        tbl_25 = 0.05 * jax.random.normal(jax.random.fold_in(_tk, 500 + 25), (1000, 32), jnp.float32)
        tbl_26 = 0.05 * jax.random.normal(jax.random.fold_in(_tk, 500 + 26), (12500, 32), jnp.float32)
        tbl_27 = 0.05 * jax.random.normal(jax.random.fold_in(_tk, 500 + 27), (12500, 32), jnp.float32)
        tbl_28 = 0.05 * jax.random.normal(jax.random.fold_in(_tk, 500 + 28), (125000, 32), jnp.float32)
        tbl_29 = 0.05 * jax.random.normal(jax.random.fold_in(_tk, 500 + 29), (12500, 32), jnp.float32)
        tbl_30 = 0.05 * jax.random.normal(jax.random.fold_in(_tk, 500 + 30), (12500, 32), jnp.float32)
        tbl_31 = 0.05 * jax.random.normal(jax.random.fold_in(_tk, 500 + 31), (1000, 32), jnp.float32)
        tbl_32 = 0.05 * jax.random.normal(jax.random.fold_in(_tk, 500 + 32), (1250, 32), jnp.float32)
        tbl_33 = 0.05 * jax.random.normal(jax.random.fold_in(_tk, 500 + 33), (1000, 32), jnp.float32)
        tbl_34 = 0.05 * jax.random.normal(jax.random.fold_in(_tk, 500 + 34), (12500, 32), jnp.float32)
        tbl_35 = 0.05 * jax.random.normal(jax.random.fold_in(_tk, 500 + 35), (12500, 32), jnp.float32)
        tbl_36 = 0.05 * jax.random.normal(jax.random.fold_in(_tk, 500 + 36), (1000, 32), jnp.float32)
        tbl_37 = 0.05 * jax.random.normal(jax.random.fold_in(_tk, 500 + 37), (1000, 32), jnp.float32)
        tbl_38 = 0.05 * jax.random.normal(jax.random.fold_in(_tk, 500 + 38), (12500, 32), jnp.float32)
        tbl_39 = 0.05 * jax.random.normal(jax.random.fold_in(_tk, 500 + 39), (1000, 32), jnp.float32)
        _rk = jax.random.fold_in(_tk, 7)
        W_top1 = 0.176777 * jax.random.normal(jax.random.fold_in(_tk, 801), (32, 512), jnp.float32)
        W_top2 = 0.0441942 * jax.random.normal(jax.random.fold_in(_tk, 802), (512, 256), jnp.float32)
        W_top3 = 0.0625 * jax.random.normal(jax.random.fold_in(_tk, 803), (256, 1), jnp.float32)
        b_top1 = jnp.zeros((512,), jnp.float32)
        b_top2 = jnp.zeros((256,), jnp.float32)
        return (dense_ctx, ids, tbl_0, tbl_1, tbl_2, tbl_3, tbl_4, tbl_5, tbl_6, tbl_7, tbl_8, tbl_9, tbl_10, tbl_11, tbl_12, tbl_13, tbl_14, tbl_15, tbl_16, tbl_17, tbl_18, tbl_19, tbl_20, tbl_21, tbl_22, tbl_23, tbl_24, tbl_25, tbl_26, tbl_27, tbl_28, tbl_29, tbl_30, tbl_31, tbl_32, tbl_33, tbl_34, tbl_35, tbl_36, tbl_37, tbl_38, tbl_39, W_top1, b_top1, W_top2, b_top2, W_top3)
    dense_ctx, ids, tbl_0, tbl_1, tbl_2, tbl_3, tbl_4, tbl_5, tbl_6, tbl_7, tbl_8, tbl_9, tbl_10, tbl_11, tbl_12, tbl_13, tbl_14, tbl_15, tbl_16, tbl_17, tbl_18, tbl_19, tbl_20, tbl_21, tbl_22, tbl_23, tbl_24, tbl_25, tbl_26, tbl_27, tbl_28, tbl_29, tbl_30, tbl_31, tbl_32, tbl_33, tbl_34, tbl_35, tbl_36, tbl_37, tbl_38, tbl_39, W_top1, b_top1, W_top2, b_top2, W_top3 = _rec_inputs()

    def _L0_rec_setup():
        import jax, jax.numpy as jnp
        import numpy as np
        import itertools
        LN_EPS = 0.001

        def _pair_indices(field_num):
            pairs = np.array(list(itertools.combinations(range(field_num), 2)), dtype=np.int32)
            return (pairs[:, 0], pairs[:, 1])
        key = jax.random.key(seed)
        ks = jax.random.split(key, 3)
        B, F, E, P, D = (256, 40, 32, 780, 16)
        x = jax.random.normal(ks[0], (B, F, E), dtype=jnp.float32)
        W = jax.random.normal(ks[1], (P, E, E), dtype=jnp.float32) * (2.0 / (E + E)) ** 0.5
        dense_w = jax.random.normal(ks[2], (P, D), dtype=jnp.float32) * (2.0 / (P + D)) ** 0.5
        dense_b = jnp.zeros((D,), dtype=jnp.float32)
        gamma = jnp.ones((D,), dtype=jnp.float32)
        beta = jnp.zeros((D,), dtype=jnp.float32)
        return {'x': x, 'W': W, 'dense_w': dense_w, 'dense_b': dense_b, 'gamma': gamma, 'beta': beta}
    _L0_rec_all = _L0_rec_setup()
    _L0_rec_in = {k: v for k, v in _L0_rec_all.items() if k in ('W', 'dense_w', 'dense_b', 'gamma', 'beta')}
    del _L0_rec_all
    return {'dense_ctx': dense_ctx, 'ids': ids, 'tbl_0': tbl_0, 'tbl_1': tbl_1, 'tbl_2': tbl_2, 'tbl_3': tbl_3, 'tbl_4': tbl_4, 'tbl_5': tbl_5, 'tbl_6': tbl_6, 'tbl_7': tbl_7, 'tbl_8': tbl_8, 'tbl_9': tbl_9, 'tbl_10': tbl_10, 'tbl_11': tbl_11, 'tbl_12': tbl_12, 'tbl_13': tbl_13, 'tbl_14': tbl_14, 'tbl_15': tbl_15, 'tbl_16': tbl_16, 'tbl_17': tbl_17, 'tbl_18': tbl_18, 'tbl_19': tbl_19, 'tbl_20': tbl_20, 'tbl_21': tbl_21, 'tbl_22': tbl_22, 'tbl_23': tbl_23, 'tbl_24': tbl_24, 'tbl_25': tbl_25, 'tbl_26': tbl_26, 'tbl_27': tbl_27, 'tbl_28': tbl_28, 'tbl_29': tbl_29, 'tbl_30': tbl_30, 'tbl_31': tbl_31, 'tbl_32': tbl_32, 'tbl_33': tbl_33, 'tbl_34': tbl_34, 'tbl_35': tbl_35, 'tbl_36': tbl_36, 'tbl_37': tbl_37, 'tbl_38': tbl_38, 'tbl_39': tbl_39, 'W_top1': W_top1, 'b_top1': b_top1, 'W_top2': W_top2, 'b_top2': b_top2, 'W_top3': W_top3, 'L0_rec_W': _L0_rec_in['W'], 'L0_rec_dense_w': _L0_rec_in['dense_w'], 'L0_rec_dense_b': _L0_rec_in['dense_b'], 'L0_rec_gamma': _L0_rec_in['gamma'], 'L0_rec_beta': _L0_rec_in['beta']}

def reference(dense_ctx, ids, tbl_0, tbl_1, tbl_2, tbl_3, tbl_4, tbl_5, tbl_6, tbl_7, tbl_8, tbl_9, tbl_10, tbl_11, tbl_12, tbl_13, tbl_14, tbl_15, tbl_16, tbl_17, tbl_18, tbl_19, tbl_20, tbl_21, tbl_22, tbl_23, tbl_24, tbl_25, tbl_26, tbl_27, tbl_28, tbl_29, tbl_30, tbl_31, tbl_32, tbl_33, tbl_34, tbl_35, tbl_36, tbl_37, tbl_38, tbl_39, W_top1, b_top1, W_top2, b_top2, W_top3, L0_rec_W, L0_rec_dense_w, L0_rec_dense_b, L0_rec_gamma, L0_rec_beta):
    import jax
    import jax.numpy as jnp

    def _L0_rec_ref(x, W, dense_w, dense_b, gamma, beta):
        import jax, jax.numpy as jnp
        import numpy as np
        import itertools
        LN_EPS = 0.001

        def _pair_indices(field_num):
            pairs = np.array(list(itertools.combinations(range(field_num), 2)), dtype=np.int32)
            return (pairs[:, 0], pairs[:, 1])
        F = x.shape[1]
        idx_i, idx_j = _pair_indices(F)
        xi = x[:, idx_i, :]
        xj = x[:, idx_j, :]
        t = jnp.einsum('bpe,pef->bpf', xi, W)
        p = jnp.einsum('bpf,bpf->bp', t, xj)
        h = p @ dense_w + dense_b
        mu = jnp.mean(h, axis=-1, keepdims=True)
        var = jnp.mean(jnp.square(h - mu), axis=-1, keepdims=True)
        out = (h - mu) * jax.lax.rsqrt(var + LN_EPS) * gamma + beta
        return out
    e = jnp.stack([tbl_0[ids[:, 0]], tbl_1[ids[:, 1]], tbl_2[ids[:, 2]], tbl_3[ids[:, 3]], tbl_4[ids[:, 4]], tbl_5[ids[:, 5]], tbl_6[ids[:, 6]], tbl_7[ids[:, 7]], tbl_8[ids[:, 8]], tbl_9[ids[:, 9]], tbl_10[ids[:, 10]], tbl_11[ids[:, 11]], tbl_12[ids[:, 12]], tbl_13[ids[:, 13]], tbl_14[ids[:, 14]], tbl_15[ids[:, 15]], tbl_16[ids[:, 16]], tbl_17[ids[:, 17]], tbl_18[ids[:, 18]], tbl_19[ids[:, 19]], tbl_20[ids[:, 20]], tbl_21[ids[:, 21]], tbl_22[ids[:, 22]], tbl_23[ids[:, 23]], tbl_24[ids[:, 24]], tbl_25[ids[:, 25]], tbl_26[ids[:, 26]], tbl_27[ids[:, 27]], tbl_28[ids[:, 28]], tbl_29[ids[:, 29]], tbl_30[ids[:, 30]], tbl_31[ids[:, 31]], tbl_32[ids[:, 32]], tbl_33[ids[:, 33]], tbl_34[ids[:, 34]], tbl_35[ids[:, 35]], tbl_36[ids[:, 36]], tbl_37[ids[:, 37]], tbl_38[ids[:, 38]], tbl_39[ids[:, 39]]], axis=1)
    z = _L0_rec_ref(e, L0_rec_W, L0_rec_dense_w, L0_rec_dense_b, L0_rec_gamma, L0_rec_beta)
    z = z.reshape(z.shape[0], -1)
    h = jnp.concatenate([z, dense_ctx], axis=1)
    h = jnp.maximum(h @ W_top1 + b_top1, 0.0)
    h = jnp.maximum(h @ W_top2 + b_top2, 0.0)
    y = h @ W_top3
    return y

_drawn_inputs = setup_inputs


def setup_inputs(seed=0):
    import zlib

    import numpy as np

    out = dict(_drawn_inputs(seed))
    spreads = {'b_top1': (0.0, 0.1),
     'b_top2': (0.0, 0.1),
     'L0_rec_dense_b': (0.0, 0.1),
     'L0_rec_gamma': (1.0, 0.2),
     'L0_rec_beta': (0.0, 0.1)}
    factors = {}
    for name, (base, spread) in spreads.items():
        noise = np.random.default_rng([zlib.crc32(name.encode()), seed]).standard_normal(out[name].shape)
        drawn = base * np.exp(spread * noise) if base else spread * noise
        out[name] = jnp.asarray(drawn.astype(out[name].dtype))
    for name, factor in factors.items():
        out[name] = (out[name] * factor).astype(out[name].dtype)
    return out
```

```python
from contextlib import ExitStack

import concourse.bass as bass
from concourse import mybir

F32 = mybir.dt.float32
F32R = mybir.dt.float32r
I32 = mybir.dt.int32
ALU = mybir.AluOpType
ACT = mybir.ActivationFunctionType

P = 128
BATCH = 2048
FIELDS = 40
E = 32
D = 16
LN_EPS = 0.001
CF = P // E
CHUNKS = FIELDS // CF
NB = 256
BT = NB // P
BLOCKS = BATCH // NB
HID1, HID2 = 512, 256
M1, M2 = HID1 // P, HID2 // P

GROUPS = [(J, I) for J in range(CHUNKS) for I in range(J + 1)]
NG = len(GROUPS)
UNITS_OF = [[CF * I + r for r in range(CF if I < J else CF - 1)] for J, I in GROUPS]
UNIT0 = [sum(len(u) for u in UNITS_OF[:g]) for g in range(NG)]
NU = sum(len(u) for u in UNITS_OF)
UNIT_LIST = [(i, J) for (J, _), us in zip(GROUPS, UNITS_OF) for i in us]
FIRST_G = [J * (J + 1) // 2 for J in range(CHUNKS + 1)]

PIECE = 5
PIECES = -(-NU // PIECE)
TR_STEPS = 3

MLP_AT = {11: "z", 17: "ct", 20: "h1a", 23: "h1b", 27: "h2", 31: "y"}


def dlrm_tower(nc, ids, tables, ctx_in, w_stack, dw_rows, sel, scale_shift, w1, b1, w2, b2, w3, ident_in, y_out):
    with ExitStack() as stack:
        def sb(name, shape, dt=F32):
            return stack.enter_context(nc.sbuf_tensor(name, shape, dt))

        def psum(name, shape):
            return stack.enter_context(nc.psum_tensor(name, shape, F32))

        def sem(name):
            return stack.enter_context(nc.semaphore(name))

        t_ps = [psum(f"t_ps{n}", [P, CF, NB]) for n in range(2)]
        h_ps = psum("h_ps", [P, 512])
        tr_ps = [psum(f"tr_ps{n}", [P, 2, NB]) for n in range(2)]
        mlp_ps = psum("mlp_ps", [P, 512])

        w_raw = sb("w_raw", [P, 2, PIECE * P])
        w_split = sb("w_split", [P, NU * P], F32R)
        dw = sb("dw", [P, NU * D])
        idx = sb("idx", [P, CHUNKS, BT * CF], I32)
        x_rows = sb("x_rows", [P, CHUNKS, BT, P])
        x_hl = sb("x_hl", [P, 2, BT * CF, 4, E], F32R)
        x_stack = sb("x_stack", [P, FIELDS, NB], F32R)
        x_cols = sb("x_cols", [P, 2, NB])
        prod = sb("prod", [P, 2, CF, NB])
        ident = sb("ident", [P, P])
        h_sb = sb("h_sb", [P, NB])
        sel_sb = sb("sel_sb", [P, D])
        stats = sb("stats", [P, BT, 6])
        mv = sb("mv", [P, BT, 2])
        var = sb("var", [P, BT])
        std = sb("std", [P, BT])
        rstd = sb("rstd", [P, BT])
        cat = sb("cat", [P, BT, 2 * D])
        ss = sb("ss", [2 * D, 2])
        cat_t = sb("cat_t", [2 * D, NB])
        w1_sb = sb("w1_sb", [2 * D, HID1])
        b1_sb = sb("b1_sb", [P, M1])
        w2_sb = sb("w2_sb", [P, M1, HID2])
        b2_sb = sb("b2_sb", [P, M2])
        w3_sb = sb("w3_sb", [P, M2])
        a1 = sb("a1", [P, M1, NB])
        a2 = sb("a2", [P, M2, NB])
        y_sb = sb("y_sb", [1, NB])

        s_const = sem("s_const")
        s_dw = sem("s_dw")
        s_raw = [sem(f"s_raw{n}") for n in range(2)]
        s_whi = sem("s_whi")
        s_w = sem("s_w")
        s_idx = [sem(f"s_idx{J}") for J in range(CHUNKS)]
        s_slot = sem("s_slot")
        s_x = [sem(f"s_x{J}") for J in range(CHUNKS)]
        s_hi = sem("s_hi")
        s_lo = sem("s_lo")
        s_hl = sem("s_hl")
        s_tr = sem("s_tr")
        s_ev = sem("s_ev")
        s_t = sem("s_t")
        s_prod = sem("s_prod")
        s_red = sem("s_red")
        s_ones = sem("s_ones")
        s_h = sem("s_h")
        s_z = sem("s_z")
        s_st = sem("s_st")
        s_carry = sem("s_carry")
        s_var = sem("s_var")
        s_std = sem("s_std")
        s_ctx = sem("s_ctx")
        s_norm = sem("s_norm")
        s_catps = sem("s_catps")
        s_cat = sem("s_cat")
        s_h1 = sem("s_h1")
        s_a1 = sem("s_a1")
        s_h2 = sem("s_h2")
        s_a2 = sem("s_a2")
        s_yps = sem("s_yps")
        s_y = sem("s_y")
        s_out = sem("s_out")

        N_CONST = 8
        block = stack.enter_context(nc.Block())

        @block.sync
        def _(sp):
            def load_ids(k, J):
                sp.dma_start(idx[:, J, :], ids[k, J]).then_inc(s_idx[J], 16)

            def load_ctx(k):
                sp.dma_start(cat[:, :, D:2 * D], ctx_in[k].rearrange("(t p) d -> p t d", p=P)).then_inc(s_ctx, 16)

            def store_y(k):
                sp.wait_ge(s_y, k + 1)
                sp.dma_start(y_out[k], y_sb[:, :]).then_inc(s_out, 16)

            for J in range(CHUNKS):
                load_ids(0, J)
            for dst, src in ((ident, ident_in), (sel_sb, sel), (ss, scale_shift), (w1_sb, w1), (b1_sb, b1),
                             (w2_sb, w2), (b2_sb, b2), (w3_sb, w3)):
                sp.dma_start(dst[:], src).then_inc(s_const, 16)
            load_ctx(0)
            for n in range(PIECES):
                cols = min(PIECE, NU - n * PIECE) * P
                if n >= 2:
                    sp.wait_ge(s_w, n - 1)
                for r in range(4):
                    sp.dma_start(w_raw[E * r:E * r + E, n % 2, 0:cols],
                                 w_stack[:, n * PIECE * P:n * PIECE * P + cols]).then_inc(s_raw[n % 2], 16)
                if n == 2:
                    for c in range(CF):
                        sp.dma_start(dw[E * c:E * c + E, :],
                                     dw_rows[c:c + 1, :].to_broadcast([E, NU * D])).then_inc(s_dw, 16)

            def body(k, first=False, last=False):
                for J in range(CHUNKS):
                    if not last:
                        sp.wait_ge(s_x[J], (k + 1) * (16 * BT * CF))
                        load_ids(k + 1, J)
                if not first:
                    store_y(k - 1)
                    sp.wait_ge(s_catps, k)
                    load_ctx(k)

            body(0, first=True)
            with sp.Fori(1, BLOCKS - 1) as k:
                body(k)
            body(BLOCKS - 1, last=True)
            store_y(BLOCKS - 1)
            sp.wait_ge(s_out, 16 * BLOCKS)

        @block.gpsimd
        def _(pool):
            def body(k, first=False):
                for J in range(CHUNKS):
                    pool.wait_ge(s_idx[J], (k + 1) * 16)
                    if not first:
                        pool.wait_ge(s_tr, k * (TR_STEPS * CHUNKS) + (TR_STEPS * (J + 1 - CHUNKS)))
                    pool.sem_inc(s_slot, 1)
                    for t in range(BT):
                        for c in range(CF):
                            pool.indirect_dma_start(
                                x_rows[:, J, t, E * c:E * c + E], None, tables[CF * J + c],
                                bass.IndirectOffsetOnAxis(ap=idx[:, J, t * CF + c:t * CF + c + 1], axis=0),
                            ).then_inc(s_x[J], 16)

            body(0, first=True)
            with pool.Fori(1, BLOCKS) as k:
                body(k)

        @block.scalar
        def _(act):
            for n in range(PIECES):
                cols = min(PIECE, NU - n * PIECE) * P
                act.wait_ge(s_raw[n % 2], 64 * (n // 2 + 1))
                nc.scalar.activation(w_split[:, n * PIECE * P:n * PIECE * P + cols], w_raw[:, n % 2, 0:cols],
                                     ACT.Copy).then_inc(s_whi, 1)

            def hi(k, J):
                act.wait_ge(s_x[J], (k + 1) * (16 * BT * CF))
                n_back = (TR_STEPS * (J - 2) + 2)
                if isinstance(k, int) and k == 0:
                    if J >= 2:
                        act.wait_ge(s_tr, n_back)
                else:
                    act.wait_ge(s_tr, k * (TR_STEPS * CHUNKS) + n_back)
                src = x_rows[:, J].rearrange("p t (c r e) -> p (t c) r e", r=1, e=E)
                nc.scalar.activation(x_hl[:, J % 2, :, 0:3:2, :], src.to_broadcast([P, BT * CF, 2, E]),
                                     ACT.Copy).then_inc(s_hi, 1)

            def repeat_lo(k, J):
                act.wait_ge(s_lo, k * CHUNKS + (J + 1))
                nc.scalar.activation(x_hl[:, J % 2, :, 3, :], x_hl[:, J % 2, :, 1, :].bitcast(F32),
                                     ACT.Copy).then_inc(s_hl, 1)

            def evac(k, J, s):
                act.wait_ge(s_tr, k * (TR_STEPS * CHUNKS) + (TR_STEPS * J + s + 1))
                if s < 2:
                    nc.scalar.activation(x_stack[:, CF * J + 2 * s:CF * J + 2 * s + 2, :], tr_ps[s][:],
                                         ACT.Copy).then_inc(s_ev, 1)
                    return
                g_done = FIRST_G[J - 1] if J >= 1 else FIRST_G[CHUNKS - 1] - NG
                if not (isinstance(k, int) and k == 0):
                    act.wait_ge(s_prod, k * NG + g_done)
                elif J >= 2:
                    act.wait_ge(s_prod, g_done)
                nc.scalar.activation(x_cols[:, J % 2, :], tr_ps[0][:, 0, :], ACT.Copy).then_inc(s_ev, 1)

            def mlp(k, step):
                if step == "std":
                    act.wait_ge(s_var, k + 1)
                    nc.scalar.activation(std[:, :], var[:, :], ACT.Sqrt).then_inc(s_std, 1)
                elif step in ("h1a", "h1b"):
                    half = int(step == "h1b")
                    act.wait_ge(s_h1, k * 2 + (half + 1))
                    for m in range(2):
                        last = nc.scalar.activation(a1[:, 2 * half + m, :], mlp_ps[:, m * NB:m * NB + NB], ACT.Relu,
                                                    bias=b1_sb[:, 2 * half + m:2 * half + m + 1])
                    last.then_inc(s_a1, 1)
                elif step == "h2":
                    act.wait_ge(s_h2, k + 1)
                    for m in range(M2):
                        last = nc.scalar.activation(a2[:, m, :], mlp_ps[:, m * NB:m * NB + NB], ACT.Relu,
                                                    bias=b2_sb[:, m:m + 1])
                    last.then_inc(s_a2, 1)
                elif step == "y":
                    act.wait_ge(s_yps, k + 1)
                    if not (isinstance(k, int) and k == 0):
                        act.wait_ge(s_out, k * 16)
                    nc.scalar.activation(y_sb[:, :], mlp_ps[0:1, 0:NB], ACT.Copy).then_inc(s_y, 1)

            def save_h(k):
                act.wait_ge(s_red, (k + 1) * NG)
                if not (isinstance(k, int) and k == 0):
                    act.wait_ge(s_z, k)
                for r in range(CF):
                    last = nc.scalar.activation(h_sb[E * r:E * r + D, :], h_ps[E * r:E * r + D, 0:NB], ACT.Copy)
                last.then_inc(s_h, 1)

            act_at = {12: "std", 20: "h1a", 23: "h1b", 27: "h2", 31: "y"}

            def body(k, first=False, last=False):
                for g, (J, I) in enumerate(GROUPS):
                    if I == 0:
                        if J + 1 < CHUNKS:
                            repeat_lo(k, J + 1)
                        elif not last:
                            repeat_lo(k + 1, 0)
                        if J + 2 < CHUNKS:
                            hi(k, J + 2)
                        elif not last:
                            hi(k + 1, J + 2 - CHUNKS)
                    for s in steps_at(J, I):
                        if J + 1 < CHUNKS:
                            evac(k, J + 1, s)
                        elif not last:
                            evac(k + 1, 0, s)
                    if not first and g in act_at:
                        mlp(k - 1, act_at[g])
                save_h(k)

            act.wait_ge(s_const, 16 * N_CONST)
            hi(0, 0)
            hi(0, 1)
            repeat_lo(0, 0)
            for s in range(TR_STEPS):
                evac(0, 0, s)
            act.wait_ge(s_ones, 1)
            body(0, first=True)
            with act.Fori(1, BLOCKS - 1) as k:
                body(k)
            body(BLOCKS - 1, last=True)
            for step in ("std", "h1a", "h1b", "h2", "y"):
                mlp(BLOCKS - 1, step)

        @block.vector
        def _(dve):
            nc.vector.memset(h_sb[:, :], 1.0).then_inc(s_ones, 1)
            for n in range(PIECES):
                cols = min(PIECE, NU - n * PIECE) * P
                w = w_split[P // 2:P, n * PIECE * P:n * PIECE * P + cols]
                dve.wait_ge(s_whi, n + 1)
                nc.vector.tensor_tensor(w, w_raw[P // 2:P, n % 2, 0:cols], w.bitcast(F32),
                                        ALU.subtract).then_inc(s_w, 1)

            def lo(k, J):
                dve.wait_ge(s_hi, k * CHUNKS + (J + 1))
                nc.vector.tensor_tensor(x_hl[:, J % 2, :, 1, :],
                                        x_rows[:, J].rearrange("p t (c e) -> p (t c) e", e=E),
                                        x_hl[:, J % 2, :, 0, :].bitcast(F32), ALU.subtract).then_inc(s_lo, 1)

            def multiply(k, g):
                J, I = GROUPS[g]
                n = len(UNITS_OF[g])
                if I == 0:
                    dve.wait_ge(s_ev, k * (TR_STEPS * CHUNKS) + TR_STEPS * (J + 1))
                dve.wait_ge(s_t, k * NG + (g + 1))
                if not (isinstance(k, int) and k == 0):
                    dve.wait_ge(s_red, k * NG + (g - 1))
                elif g >= 2:
                    dve.wait_ge(s_red, g - 1)
                xj = x_cols[:, J % 2, :].rearrange("p (u b) -> p u b", u=1).to_broadcast([P, n, NB])
                slot = g % 2
                nc.vector.tensor_tensor(prod[:, slot, 0:n, :], t_ps[slot][:, 0:n, :], xj,
                                        ALU.mult).then_inc(s_prod, 1)

            def mlp(k, step):
                z = mlp_ps[:, 0:BT * D].rearrange("p (t d) -> p t d", d=D)
                if step == "stats":
                    dve.wait_ge(s_z, k + 1)
                    for t in range(BT):
                        last = nc.vector.bn_stats(stats[:, t, :], z[:, t, :])
                    last.then_inc(s_st, 1)
                    dve.wait_ge(s_st, k * 3 + 1)
                    dve.sem_inc(s_carry, 1)
                    for t in range(BT):
                        last = nc.vector.bn_aggr(mv[:, t, :], stats[:, t, :])
                    last.then_inc(s_st, 1)
                    dve.wait_ge(s_st, k * 3 + 2)
                    nc.vector.tensor_scalar(var[:, :], mv[:, :, 1], LN_EPS, None, ALU.add).then_inc(s_var, 1)
                elif step == "norm":
                    dve.wait_ge(s_std, k + 1)
                    nc.vector.reciprocal(rstd[:, :], std[:, :]).then_inc(s_st, 1)
                    dve.wait_ge(s_st, k * 3 + 3)
                    if not (isinstance(k, int) and k == 0):
                        dve.wait_ge(s_catps, k)
                    for t in range(BT):
                        last = nc.vector.tensor_scalar(cat[:, t, 0:D], z[:, t, :], mv[:, t, 0:1], rstd[:, t:t + 1],
                                                       ALU.subtract, ALU.mult)
                    last.then_inc(s_norm, 1)
                elif step == "cat":
                    dve.wait_ge(s_catps, k + 1)
                    nc.vector.tensor_scalar(cat_t[:, :], mlp_ps[0:2 * D, 0:NB], ss[:, 0:1], ss[:, 1:2],
                                            ALU.mult, ALU.add).then_inc(s_cat, 1)

            dve_at = {12: "stats", 14: "norm", 18: "cat"}

            def body(k, first=False, last=False):
                for g, (J, I) in enumerate(GROUPS):
                    if I == 0:
                        if J + 2 < CHUNKS:
                            lo(k, J + 2)
                        elif not last:
                            lo(k + 1, J + 2 - CHUNKS)
                    multiply(k, g)
                    if not first and g in dve_at:
                        mlp(k - 1, dve_at[g])

            dve.wait_ge(s_const, 16 * N_CONST)
            lo(0, 0)
            lo(0, 1)
            body(0, first=True)
            with dve.Fori(1, BLOCKS - 1) as k:
                body(k)
            body(BLOCKS - 1, last=True)
            for step in ("stats", "norm", "cat"):
                mlp(BLOCKS - 1, step)

        @block.tensor
        def _(pe):
            def transposes(k, J, s):
                if s == 0:
                    pe.wait_ge(s_hl, k * CHUNKS + (J + 1))
                free = TR_STEPS * J + (0, -1, 1)[s]
                if free > 0 or not (isinstance(k, int) and k == 0):
                    pe.wait_ge(s_ev, k * (TR_STEPS * CHUNKS) + free)
                for t in range(BT):
                    rows = slice(t * P, t * P + P)
                    if s < 2:
                        for c in (2 * s, 2 * s + 1):
                            src = x_hl[:, J % 2, t * CF + c, :, :].bitcast(F32).rearrange("p r e -> p (r e)")
                            last = nc.tensor.transpose(tr_ps[s][:, c % 2, rows], src, ident[:, :])
                    else:
                        last = nc.tensor.transpose(tr_ps[0][:, 0, rows], x_rows[:, J, t, :], ident[:, :])
                last.then_inc(s_tr, 1)

            def interact(k, g):
                J, I = GROUPS[g]
                if I == J:
                    pe.wait_ge(s_ev, k * (TR_STEPS * CHUNKS) + (TR_STEPS * J + 2))
                if isinstance(k, int) and k == 0:
                    pe.wait_ge(s_w, (UNIT0[g] + len(UNITS_OF[g]) - 1) // PIECE + 1)
                    if g >= 2:
                        pe.wait_ge(s_prod, g - 1)
                else:
                    pe.wait_ge(s_prod, k * NG + (g - 1))
                for r, i in enumerate(UNITS_OF[g]):
                    u = UNIT0[g] + r
                    last = nc.tensor.matmul(t_ps[g % 2][:, r, :], w_split[:, u * P:u * P + P], x_stack[:, i, :],
                                            start=True, stop=True)
                last.then_inc(s_t, 1)

            def reduce(k, g):
                pe.wait_ge(s_prod, k * NG + (g + 1))
                if g == 0:
                    if isinstance(k, int) and k == 0:
                        pe.wait_ge(s_dw, 16 * CF)
                    else:
                        pe.wait_ge(s_h, k)
                for r in range(len(UNITS_OF[g])):
                    u = UNIT0[g] + r
                    final = NG - 1 if r < CF - 1 else NG - 2
                    begin = 0 if r < CF - 1 else 1
                    last = nc.tensor.matmul(h_ps[E * r:E * r + D, 0:NB], dw[:, u * D:u * D + D], prod[:, g % 2, r, :],
                                            start=(g == begin), stop=(g == final), tile_position=(0, E * r))
                last.then_inc(s_red, 1)

            def mlp(k, step):
                if step == "z":
                    pe.wait_ge(s_h, k + 1)
                    if not (isinstance(k, int) and k == 0):
                        pe.wait_ge(s_y, k)
                    for t in range(BT):
                        last = nc.tensor.matmul(mlp_ps[:, t * D:t * D + D], h_sb[:, t * P:t * P + P], sel_sb[:, :],
                                                start=True, stop=True)
                    last.then_inc(s_z, 1)
                elif step == "ct":
                    pe.wait_ge(s_norm, k + 1)
                    pe.wait_ge(s_ctx, k * 16 + 16)
                    for t in range(BT):
                        last = nc.tensor.transpose(mlp_ps[0:2 * D, t * P:t * P + P], cat[:, t, :], ident[:, :])
                    last.then_inc(s_catps, 1)
                elif step in ("h1a", "h1b"):
                    half = int(step == "h1b")
                    if half:
                        pe.wait_ge(s_a1, k * 2 + 1)
                    else:
                        pe.wait_ge(s_cat, k + 1)
                    for m in range(2):
                        c = (2 * half + m) * P
                        last = nc.tensor.matmul(mlp_ps[:, m * NB:m * NB + NB], w1_sb[:, c:c + P], cat_t[:, :],
                                                start=True, stop=True)
                    last.then_inc(s_h1, 1)
                elif step == "h2":
                    pe.wait_ge(s_a1, k * 2 + 2)
                    for m in range(M2):
                        for q in range(M1):
                            last = nc.tensor.matmul(mlp_ps[:, m * NB:m * NB + NB], w2_sb[:, q, m * P:m * P + P],
                                                    a1[:, q, :], start=(q == 0), stop=(q == M1 - 1))
                    last.then_inc(s_h2, 1)
                elif step == "y":
                    pe.wait_ge(s_a2, k + 1)
                    for q in range(M2):
                        last = nc.tensor.matmul(mlp_ps[0:1, 0:NB], w3_sb[:, q:q + 1], a2[:, q, :],
                                                start=(q == 0), stop=(q == M2 - 1))
                    last.then_inc(s_yps, 1)

            def body(k, first=False, last=False):
                for g, (J, I) in enumerate(GROUPS):
                    for s in steps_at(J, I):
                        if J + 1 < CHUNKS:
                            transposes(k, J + 1, s)
                        elif not last:
                            transposes(k + 1, 0, s)
                    for n in AHEAD[g]:
                        interact(k, n)
                    reduce(k, g)
                    if not first and g in MLP_AT:
                        mlp(k - 1, MLP_AT[g])

            pe.wait_ge(s_const, 16 * N_CONST)
            for s in range(TR_STEPS):
                transposes(0, 0, s)
            body(0, first=True)
            with pe.Fori(1, BLOCKS - 1) as k:
                body(k)
            body(BLOCKS - 1, last=True)
            for step in ("z", "ct", "h1a", "h1b", "h2", "y"):
                mlp(BLOCKS - 1, step)


def steps_at(J, I):
    start = min(1, J)
    if J < TR_STEPS:
        return range(TR_STEPS) if I == 0 else ()
    return (I - start,) if start <= I < start + TR_STEPS else ()


AHEAD = [[0, 1, 2] if g == 0 else [g + 2] if g + 2 < NG else [] for g in range(NG)]


_TABLES = [f"tbl_{f}" for f in range(FIELDS)]


def kernel(**inputs):
    import numpy as np
    import concourse.bacc as bacc
    from concourse.bass_utils import run_bass_kernel_spmd

    nc = bacc.Bacc("TRN2", target_bir_lowering=False, num_devices=1)
    x = {n: np.ascontiguousarray(a) for n, a in inputs.items()}
    ids = x["ids"].reshape(BLOCKS, BT, P, CHUNKS, CF).transpose(0, 3, 2, 1, 4).reshape(BLOCKS, CHUNKS, P, BT * CF)

    pair = {}
    for i in range(FIELDS):
        for j in range(i + 1, FIELDS):
            pair[i, j] = len(pair)
    none = len(pair)
    rows = np.array([[pair.get((i, CF * J + c), none) for c in range(CF)] for i, J in UNIT_LIST])
    w_pad = np.concatenate([x["L0_rec_W"], np.zeros((1, E, E), np.float32)])
    w_stack = w_pad[rows].transpose(2, 0, 1, 3).reshape(E, NU * P)
    dw_pad = np.concatenate([x["L0_rec_dense_w"], np.zeros((1, D), np.float32)])
    dw_rows = dw_pad[rows].transpose(1, 0, 2).reshape(CF, NU * D)
    sel = np.zeros((P, D), np.float32)
    for r in range(CF):
        sel[E * r:E * r + D] = np.eye(D, dtype=np.float32)
    sel[D] = x["L0_rec_dense_b"]
    scale_shift = np.stack([np.concatenate([x["L0_rec_gamma"], np.ones(D, np.float32)]),
                            np.concatenate([x["L0_rec_beta"], np.zeros(D, np.float32)])], axis=1)
    arrays = {
        "ids_in": ids,
        **{n: x[n] for n in _TABLES},
        "ctx_in": x["dense_ctx"].reshape(BLOCKS, NB, D),
        "w_stack": w_stack, "dw_rows": dw_rows, "sel": sel, "scale_shift": scale_shift,
        "w1": x["W_top1"], "b1": x["b_top1"].reshape(M1, P).T,
        "w2": x["W_top2"].reshape(M1, P, HID2).transpose(1, 0, 2), "b2": x["b_top2"].reshape(M2, P).T,
        "w3": x["W_top3"].reshape(M2, P).T, "ident": np.eye(P, dtype=np.float32),
    }
    arrays = {n: np.ascontiguousarray(a) for n, a in arrays.items()}
    dram = {n: nc.dram_tensor(f"{n}_dram", a.shape, mybir.dt.from_np(a.dtype), kind="ExternalInput").ap()
            for n, a in arrays.items()}
    y = nc.dram_tensor("y", (BLOCKS, 1, NB), F32, kind="ExternalOutput").ap()
    dlrm_tower(nc, dram["ids_in"], [dram[n] for n in _TABLES], dram["ctx_in"], dram["w_stack"], dram["dw_rows"],
               dram["sel"], dram["scale_shift"], dram["w1"], dram["b1"], dram["w2"], dram["b2"], dram["w3"],
               dram["ident"], y)
    r = run_bass_kernel_spmd(nc, [{f"{n}_dram": a for n, a in arrays.items()}], core_ids=[0])
    return r.results[0]["y"].reshape(BATCH, 1)
```

```python
from contextlib import ExitStack

import concourse.bass as bass
from concourse import mybir

F32 = mybir.dt.float32
F32R = mybir.dt.float32r
I32 = mybir.dt.int32
ALU = mybir.AluOpType
ACT = mybir.ActivationFunctionType

P = 128
BATCH = 2048
FIELDS = 40
E = 32
D = 16
LN_EPS = 0.001
CF = P // E
CHUNKS = FIELDS // CF
NB = 256
BT = NB // P
BLOCKS = BATCH // NB
HID1, HID2 = 512, 256
M1, M2 = HID1 // P, HID2 // P

GROUPS = [(J, I) for J in range(CHUNKS) for I in range(J + 1)]
UNITS_OF = [[CF * I + r for r in range(CF if I < J else CF - 1)] for J, I in GROUPS]
GROUPS.append(GROUPS[-1])
UNITS_OF[-1:] = [UNITS_OF[-1][:2], UNITS_OF[-1][2:]]
NG = len(GROUPS)
T_RING, PROD_RING, ROWS_RING = 2, 4, 5
assert NG % T_RING == 0 and NG % PROD_RING == 0 and CHUNKS % ROWS_RING == 0
UNIT0 = [sum(len(u) for u in UNITS_OF[:g]) for g in range(NG)]
NU = sum(len(u) for u in UNITS_OF)
UNIT_LIST = [(i, J) for (J, _), us in zip(GROUPS, UNITS_OF) for i in us]
TILE_GROUPS = [[g for g in range(NG) if any(i % CF == tile for i in UNITS_OF[g])] for tile in range(CF)]
FIRST_G = [J * (J + 1) // 2 for J in range(CHUNKS)] + [NG]

PIECE = 4
RING = 4
PIECES = -(-NU // PIECE)
LEAD = 6

PREP_AT = {}
for _J in range(CHUNKS):
    if _J < 3:
        _steps = {"round": FIRST_G[CHUNKS - 1] + 3 * _J - 1, "sub": FIRST_G[CHUNKS - 1] + 3 * _J + 1,
                  "plain": FIRST_G[CHUNKS - 1] + 3 * _J + 2, "pairs": FIRST_G[CHUNKS - 1] + 3 * _J + 3}
    elif _J < 5:
        _steps = {"round": FIRST_G[_J - 1] - 3, "sub": FIRST_G[_J - 1] - 1,
                  "plain": FIRST_G[_J - 1], "pairs": FIRST_G[_J - 1] + 1}
    else:
        _steps = {"round": FIRST_G[_J - 1] - 2, "sub": FIRST_G[_J - 1],
                  "plain": FIRST_G[_J - 1] + 1, "pairs": FIRST_G[_J - 1] + 2}
    for _what, _g in _steps.items():
        PREP_AT.setdefault(_g, []).append((_what, _J))
COLS_SLOT = [J if J < 3 else 3 - (J + 1) % 2 for J in range(CHUNKS)]
COLS_BEFORE = [(1, 0), (1, 1), (1, CHUNKS - 2), (1, CHUNKS - 1), (0, 2)] + [(0, J - 2) for J in range(5, CHUNKS)]

MLP_PE = {10: "z", 16: "ct", 19: "h1a", 22: "h1b", 25: "h2-0", 27: "h2-1", 29: "h2-2", 31: "h2-3", 34: "y"}
MLP_ACT = {12: "std", 20: "h1a", 23: "h1b", 32: "h2", 35: "y"}
MLP_DVE = {12: "stats", 14: "norm", 18: "cat"}


def prep_steps(k, g, first, last):
    for what, J in PREP_AT.get(g, ()):
        ahead = J < 3
        if not (ahead and last):
            yield what, (k + 1 if ahead else k), J


def dlrm_tower(nc, ids, tables, ctx_in, w_stack, dw_rows, sel, scale_shift, w1, b1, w2, b2, w3, ident_in, y_out):
    with ExitStack() as stack:
        def sb(name, shape, dt=F32):
            return stack.enter_context(nc.sbuf_tensor(name, shape, dt))

        def psum(name, shape):
            return stack.enter_context(nc.psum_tensor(name, shape, F32))

        def sem(name):
            return stack.enter_context(nc.semaphore(name))

        t_ps = [psum(f"t_ps{n}", [P, CF, NB]) for n in range(T_RING)]
        h_ps = psum("h_ps", [P, 512])
        pair_ps = psum("pair_ps", [P, CF // 2, NB])
        plain_ps = psum("plain_ps", [P, 512])
        mlp_ps = psum("mlp_ps", [P, 512])

        w_raw = sb("w_raw", [P, RING, PIECE * P])
        w_split = sb("w_split", [P, NU * P], F32R)
        dw = sb("dw", [P, NU * D])
        idx = sb("idx", [P, CHUNKS, BT * CF], I32)
        x_rows = sb("x_rows", [P, ROWS_RING, BT, P])
        x_hl = sb("x_hl", [P, 2, BT * CF, 2, E], F32R)
        x_stack = sb("x_stack", [P, FIELDS, NB], F32R)
        x_cols = sb("x_cols", [P, 4, NB])
        prod = sb("prod", [P, PROD_RING, CF, NB])
        ident = sb("ident", [P, P])
        ident_r = sb("ident_r", [P, P], F32R)
        h_sb = sb("h_sb", [P, NB])
        sel_sb = sb("sel_sb", [P, D])
        stats = sb("stats", [P, BT, 6])
        mv = sb("mv", [P, BT, 2])
        var = sb("var", [P, BT])
        std = sb("std", [P, BT])
        rstd = sb("rstd", [P, BT])
        cat = sb("cat", [P, BT, 2 * D])
        ss = sb("ss", [2 * D, 2])
        cat_t = sb("cat_t", [2 * D, NB])
        w1_sb = sb("w1_sb", [2 * D, HID1])
        b1_sb = sb("b1_sb", [P, M1])
        w2_sb = sb("w2_sb", [P, M1, HID2])
        b2_sb = sb("b2_sb", [P, M2])
        w3_sb = sb("w3_sb", [P, M2])
        assert RING * PIECE * P >= (M1 + M2) * NB
        mlp_sb = w_raw[:, :, :].rearrange("p r c -> p (r c)")
        a1 = mlp_sb[:, 0:M1 * NB].rearrange("p (m b) -> p m b", b=NB)
        a2 = mlp_sb[:, M1 * NB:(M1 + M2) * NB].rearrange("p (m b) -> p m b", b=NB)
        y_sb = sb("y_sb", [1, NB])

        s_const = sem("s_const")
        s_dw = sem("s_dw")
        s_raw = [sem(f"s_raw{n}") for n in range(RING)]
        s_whi = sem("s_whi")
        s_w = sem("s_w")
        s_idx = [sem(f"s_idx{J}") for J in range(CHUNKS)]
        s_slot = sem("s_slot")
        s_x = [sem(f"s_x{n}") for n in range(ROWS_RING)]
        s_hi = sem("s_hi")
        s_hl = sem("s_hl")
        s_pair = sem("s_pair")
        s_stack = sem("s_stack")
        s_plain = sem("s_plain")
        s_cols = sem("s_cols")
        s_ident = sem("s_ident")
        s_t = sem("s_t")
        s_prod = sem("s_prod")
        s_red = sem("s_red")
        s_ones = sem("s_ones")
        s_h = sem("s_h")
        s_z = sem("s_z")
        s_st = sem("s_st")
        s_carry = sem("s_carry")
        s_var = sem("s_var")
        s_std = sem("s_std")
        s_ctx = sem("s_ctx")
        s_norm = sem("s_norm")
        s_catps = sem("s_catps")
        s_cat = sem("s_cat")
        s_h1 = sem("s_h1")
        s_a1 = sem("s_a1")
        s_h2 = sem("s_h2")
        s_a2 = sem("s_a2")
        s_yps = sem("s_yps")
        s_y = sem("s_y")
        s_out = sem("s_out")

        N_CONST = 8
        GATHERED = 16 * BT * CF
        TURNS = CHUNKS // ROWS_RING

        def gathered(k, J):
            return k * (TURNS * GATHERED) + (J // ROWS_RING + 1) * GATHERED

        block = stack.enter_context(nc.Block())

        @block.sync
        def _(sp):
            def load_ids(k, J):
                sp.dma_start(idx[:, J, :], ids[k, J]).then_inc(s_idx[J], 16)

            def load_ctx(k):
                sp.dma_start(cat[:, :, D:2 * D], ctx_in[k].rearrange("(t p) d -> p t d", p=P)).then_inc(s_ctx, 16)

            def store_y(k):
                sp.wait_ge(s_y, k + 1)
                sp.dma_start(y_out[k], y_sb[:, :]).then_inc(s_out, 16)

            for J in range(CHUNKS):
                load_ids(0, J)
            for dst, src in ((ident, ident_in), (sel_sb, sel), (ss, scale_shift), (w1_sb, w1), (b1_sb, b1),
                             (w2_sb, w2), (b2_sb, b2), (w3_sb, w3)):
                sp.dma_start(dst[:], src).then_inc(s_const, 16)
            load_ctx(0)

            def load_weights(n):
                cols = min(PIECE, NU - n * PIECE) * P
                if n >= RING:
                    sp.wait_ge(s_w, n - RING + 1)
                src = w_stack[:, n * PIECE * P:n * PIECE * P + cols].rearrange("(r e) c -> r e c", r=1)
                sp.dma_start(w_raw[:, n % RING, 0:cols], src.to_broadcast([4, E, cols])).then_inc(s_raw[n % RING], 16)

            n = 0
            for J in range(CHUNKS):
                while n < PIECES and n * PIECE < UNIT0[FIRST_G[min(J + 4, CHUNKS - 1)]] + CF:
                    load_weights(n)
                    n += 1
                if J == 0:
                    for c in range(CF):
                        sp.dma_start(dw[E * c:E * c + E, :],
                                     dw_rows[c:c + 1, :].to_broadcast([E, NU * D])).then_inc(s_dw, 16)
                sp.wait_ge(s_x[J % ROWS_RING], gathered(0, J))
                load_ids(1, J)
            while n < PIECES:
                load_weights(n)
                n += 1

            def body(k, first=False, last=False):
                for J in range(CHUNKS):
                    if not (first or last):
                        sp.wait_ge(s_x[J % ROWS_RING], gathered(k, J))
                        load_ids(k + 1, J)
                if not first:
                    store_y(k - 1)
                    sp.wait_ge(s_catps, k)
                    load_ctx(k)

            body(0, first=True)
            with sp.Fori(1, BLOCKS - 1) as k:
                body(k)
            body(BLOCKS - 1, last=True)
            store_y(BLOCKS - 1)
            sp.wait_ge(s_out, 16 * BLOCKS)

        @block.gpsimd
        def _(pool):
            def body(k, first=False):
                for J in range(CHUNKS):
                    pool.wait_ge(s_idx[J], (k + 1) * 16)
                    if not first or J >= ROWS_RING:
                        pool.wait_ge(s_plain, k * CHUNKS + (J + 1 - ROWS_RING))
                    pool.sem_inc(s_slot, 1)
                    for t in range(BT):
                        for c in range(CF):
                            pool.indirect_dma_start(
                                x_rows[:, J % ROWS_RING, t, E * c:E * c + E], None, tables[CF * J + c],
                                bass.IndirectOffsetOnAxis(ap=idx[:, J, t * CF + c:t * CF + c + 1], axis=0),
                            ).then_inc(s_x[J % ROWS_RING], 16)

            body(0, first=True)
            with pool.Fori(1, BLOCKS) as k:
                body(k)

        @block.scalar
        def _(act):
            def round_weights(n):
                cols = min(PIECE, NU - n * PIECE) * P
                act.wait_ge(s_raw[n % RING], 16 * (n // RING + 1))
                nc.scalar.activation(w_split[:, n * PIECE * P:n * PIECE * P + cols], w_raw[:, n % RING, 0:cols],
                                     ACT.Copy).then_inc(s_whi, 1)

            def prep(what, k, J):
                if what == "round":
                    act.wait_ge(s_x[J % ROWS_RING], gathered(k, J))
                    if J >= 2 or not (isinstance(k, int) and k == 0):
                        act.wait_ge(s_pair, k * CHUNKS + (J - 1))
                    nc.scalar.activation(x_hl[:, J % 2, :, 0, :],
                                         x_rows[:, J % ROWS_RING].rearrange("p t (c e) -> p (t c) e", e=E),
                                         ACT.Copy).then_inc(s_hi, 1)
                elif what == "pairs":
                    act.wait_ge(s_pair, k * CHUNKS + (J + 1))
                    for c in range(2):
                        for half in range(2):
                            last = nc.scalar.activation(
                                x_stack[P // 2 * half:P // 2 * (half + 1), CF * J + c:CF * J + CF:2, :],
                                pair_ps[P // 2 * c:P // 2 * (c + 1), :, :], ACT.Copy)
                    last.then_inc(s_stack, 1)
                elif what == "plain":
                    act.wait_ge(s_plain, k * CHUNKS + (J + 1))
                    back, chunk = COLS_BEFORE[J]
                    if not (isinstance(k, int) and k < back):
                        act.wait_ge(s_prod, k * NG + (FIRST_G[chunk + 1] - back * NG))
                    nc.scalar.activation(x_cols[:, COLS_SLOT[J], :], plain_ps[:, 0:NB], ACT.Copy).then_inc(s_cols, 1)

            def mlp(k, step):
                if step == "std":
                    act.wait_ge(s_var, k + 1)
                    nc.scalar.activation(std[:, :], var[:, :], ACT.Sqrt).then_inc(s_std, 1)
                elif step in ("h1a", "h1b"):
                    half = int(step == "h1b")
                    act.wait_ge(s_h1, k * 2 + (half + 1))
                    for m in range(2):
                        last = nc.scalar.activation(a1[:, 2 * half + m, :], mlp_ps[:, m * NB:m * NB + NB], ACT.Relu,
                                                    bias=b1_sb[:, 2 * half + m:2 * half + m + 1])
                    last.then_inc(s_a1, 1)
                elif step == "h2":
                    act.wait_ge(s_h2, k + 1)
                    for m in range(M2):
                        last = nc.scalar.activation(a2[:, m, :], mlp_ps[:, m * NB:m * NB + NB], ACT.Relu,
                                                    bias=b2_sb[:, m:m + 1])
                    last.then_inc(s_a2, 1)
                elif step == "y":
                    act.wait_ge(s_yps, k + 1)
                    if not (isinstance(k, int) and k == 0):
                        act.wait_ge(s_out, k * 16)
                    nc.scalar.activation(y_sb[:, :], mlp_ps[0:1, 0:NB], ACT.Copy).then_inc(s_y, 1)

            def save_h(k):
                act.wait_ge(s_red, (k + 1) * NG)
                if not (isinstance(k, int) and k == 0):
                    act.wait_ge(s_z, k)
                nc.scalar.activation(h_sb[:, :], h_ps[:, 0:NB], ACT.Copy).then_inc(s_h, 1)

            def body(k, first=False, last=False):
                for g in range(NG):
                    if first:
                        for n in pieces_at(g):
                            round_weights(n)
                    for step in prep_steps(k, g, first, last):
                        prep(*step)
                    if not first and g in MLP_ACT:
                        mlp(k - 1, MLP_ACT[g])
                save_h(k)

            act.wait_ge(s_const, 16 * N_CONST)
            nc.scalar.activation(ident_r[:, :], ident[:, :], ACT.Copy).then_inc(s_ident, 1)
            for n in pieces_at(-1):
                round_weights(n)
            for step in PROLOGUE:
                prep(*step)
            body(0, first=True)
            with act.Fori(1, BLOCKS - 1) as k:
                body(k)
            body(BLOCKS - 1, last=True)
            for step in ("std", "h1a", "h1b", "h2", "y"):
                mlp(BLOCKS - 1, step)

        @block.vector
        def _(dve):
            nc.vector.memset(h_ps[:, 0:NB], 1.0).then_inc(s_ones, 1)

            def split_weights(n):
                cols = min(PIECE, NU - n * PIECE) * P
                w = w_split[P // 2:P, n * PIECE * P:n * PIECE * P + cols]
                dve.wait_ge(s_whi, n + 1)
                nc.vector.tensor_tensor(w, w_raw[P // 2:P, n % RING, 0:cols], w.bitcast(F32),
                                        ALU.subtract).then_inc(s_w, 1)

            def prep(what, k, J):
                if what == "sub":
                    dve.wait_ge(s_hi, k * CHUNKS + (J + 1))
                    nc.vector.tensor_tensor(x_hl[:, J % 2, :, 1, :],
                                            x_rows[:, J % ROWS_RING].rearrange("p t (c e) -> p (t c) e", e=E),
                                            x_hl[:, J % 2, :, 0, :].bitcast(F32), ALU.subtract).then_inc(s_hl, 1)

            def multiply(k, g):
                J, I = GROUPS[g]
                n = len(UNITS_OF[g])
                if I == 0:
                    dve.wait_ge(s_cols, k * CHUNKS + (J + 1))
                dve.wait_ge(s_t, k * NG + (g + 1))
                if g >= PROD_RING or not (isinstance(k, int) and k == 0):
                    dve.wait_ge(s_red, k * NG + (g + 1 - PROD_RING))
                xj = x_cols[:, COLS_SLOT[J], :].rearrange("p (u b) -> p u b", u=1).to_broadcast([P, n, NB])
                nc.vector.tensor_tensor(prod[:, g % PROD_RING, 0:n, :], t_ps[g % T_RING][:, 0:n, :], xj,
                                        ALU.mult).then_inc(s_prod, 1)

            def mlp(k, step):
                z = mlp_ps[:, 0:BT * D].rearrange("p (t d) -> p t d", d=D)
                if step == "stats":
                    dve.wait_ge(s_z, k + 1)
                    for t in range(BT):
                        last = nc.vector.bn_stats(stats[:, t, :], z[:, t, :])
                    last.then_inc(s_st, 1)
                    dve.wait_ge(s_st, k * 3 + 1)
                    dve.sem_inc(s_carry, 1)
                    for t in range(BT):
                        last = nc.vector.bn_aggr(mv[:, t, :], stats[:, t, :])
                    last.then_inc(s_st, 1)
                    dve.wait_ge(s_st, k * 3 + 2)
                    nc.vector.tensor_scalar(var[:, :], mv[:, :, 1], LN_EPS, None, ALU.add).then_inc(s_var, 1)
                elif step == "norm":
                    dve.wait_ge(s_std, k + 1)
                    nc.vector.reciprocal(rstd[:, :], std[:, :]).then_inc(s_st, 1)
                    dve.wait_ge(s_st, k * 3 + 3)
                    if not (isinstance(k, int) and k == 0):
                        dve.wait_ge(s_catps, k)
                    for t in range(BT):
                        last = nc.vector.tensor_scalar(cat[:, t, 0:D], z[:, t, :], mv[:, t, 0:1], rstd[:, t:t + 1],
                                                       ALU.subtract, ALU.mult)
                    last.then_inc(s_norm, 1)
                elif step == "cat":
                    dve.wait_ge(s_catps, k + 1)
                    nc.vector.tensor_scalar(cat_t[:, :], mlp_ps[0:2 * D, 0:NB], ss[:, 0:1], ss[:, 1:2],
                                            ALU.mult, ALU.add).then_inc(s_cat, 1)

            def body(k, first=False, last=False):
                for g in range(NG):
                    if first:
                        for n in pieces_at(g):
                            split_weights(n)
                    multiply(k, g)
                    for step in prep_steps(k, g, first, last):
                        prep(*step)
                    if not first and g in MLP_DVE:
                        mlp(k - 1, MLP_DVE[g])

            dve.wait_ge(s_const, 16 * N_CONST)
            for n in pieces_at(-1):
                split_weights(n)
            for step in PROLOGUE:
                prep(*step)
            body(0, first=True)
            with dve.Fori(1, BLOCKS - 1) as k:
                body(k)
            body(BLOCKS - 1, last=True)
            for step in ("stats", "norm", "cat"):
                mlp(BLOCKS - 1, step)

        @block.tensor
        def _(pe):
            def prep(what, k, J):
                again = not (isinstance(k, int) and k == 0)
                if what == "pairs":
                    if J or again:
                        pe.wait_ge(s_stack, k * CHUNKS + J)
                    for q in range(CF // 2):
                        for t in range(BT):
                            two = x_hl[:, J % 2, t * CF + 2 * q:t * CF + 2 * q + 2, :, :].rearrange("p c h e -> p (c h e)")
                            last = nc.tensor.matmul(pair_ps[:, q, t * P:t * P + P], two, ident_r[:, :],
                                                    start=True, stop=True)
                    last.then_inc(s_pair, 1)
                elif what == "plain":
                    pe.wait_ge(s_hl, k * CHUNKS + (J + 1))
                    if J or again:
                        pe.wait_ge(s_cols, k * CHUNKS + J)
                    for t in range(BT):
                        last = nc.tensor.transpose(plain_ps[:, t * P:t * P + P], x_rows[:, J % ROWS_RING, t, :], ident[:, :])
                    last.then_inc(s_plain, 1)

            def interact(k, g):
                J, I = GROUPS[g]
                if I == J:
                    pe.wait_ge(s_stack, k * CHUNKS + (J + 1))
                if isinstance(k, int) and k == 0:
                    pe.wait_ge(s_w, (UNIT0[g] + len(UNITS_OF[g]) - 1) // PIECE + 1)
                if g >= T_RING or not (isinstance(k, int) and k == 0):
                    pe.wait_ge(s_prod, k * NG + (g + 1 - T_RING))
                for r, i in enumerate(UNITS_OF[g]):
                    u = UNIT0[g] + r
                    last = nc.tensor.matmul(t_ps[g % T_RING][:, r, :], w_split[:, u * P:u * P + P], x_stack[:, i, :],
                                            start=True, stop=True)
                last.then_inc(s_t, 1)

            def reduce(k, g):
                pe.wait_ge(s_prod, k * NG + (g + 1))
                if g == 0:
                    if isinstance(k, int) and k == 0:
                        pe.wait_ge(s_dw, 16 * CF)
                        pe.wait_ge(s_ones, 1)
                    else:
                        pe.wait_ge(s_h, k)
                for r, i in enumerate(UNITS_OF[g]):
                    u, tile = UNIT0[g] + r, i % CF
                    last = nc.tensor.matmul(h_ps[E * tile:E * tile + D, 0:NB], dw[:, u * D:u * D + D],
                                            prod[:, g % PROD_RING, r, :], start=(g == TILE_GROUPS[tile][0]),
                                            stop=(g == TILE_GROUPS[tile][-1]), tile_position=(0, E * tile))
                last.then_inc(s_red, 1)

            def mlp(k, step):
                if step == "z":
                    pe.wait_ge(s_h, k + 1)
                    if not (isinstance(k, int) and k == 0):
                        pe.wait_ge(s_y, k)
                    for t in range(BT):
                        last = nc.tensor.matmul(mlp_ps[:, t * D:t * D + D], h_sb[:, t * P:t * P + P], sel_sb[:, :],
                                                start=True, stop=True)
                    last.then_inc(s_z, 1)
                elif step == "ct":
                    pe.wait_ge(s_norm, k + 1)
                    pe.wait_ge(s_ctx, k * 16 + 16)
                    for t in range(BT):
                        last = nc.tensor.transpose(mlp_ps[0:2 * D, t * P:t * P + P], cat[:, t, :], ident[:, :])
                    last.then_inc(s_catps, 1)
                elif step in ("h1a", "h1b"):
                    half = int(step == "h1b")
                    if half:
                        pe.wait_ge(s_a1, k * 2 + 1)
                    else:
                        pe.wait_ge(s_cat, k + 1)
                    for m in range(2):
                        c = (2 * half + m) * P
                        last = nc.tensor.matmul(mlp_ps[:, m * NB:m * NB + NB], w1_sb[:, c:c + P], cat_t[:, :],
                                                start=True, stop=True)
                    last.then_inc(s_h1, 1)
                elif step.startswith("h2"):
                    m, part = divmod(int(step[-1]), 2)
                    if step == "h2-0":
                        pe.wait_ge(s_a1, k * 2 + 2)
                    for q in range(part * M1 // 2, (part + 1) * M1 // 2):
                        last = nc.tensor.matmul(mlp_ps[:, m * NB:m * NB + NB], w2_sb[:, q, m * P:m * P + P],
                                                a1[:, q, :], start=(q == 0), stop=(q == M1 - 1))
                    if step == "h2-3":
                        last.then_inc(s_h2, 1)
                elif step == "y":
                    pe.wait_ge(s_a2, k + 1)
                    for q in range(M2):
                        last = nc.tensor.matmul(mlp_ps[0:1, 0:NB], w3_sb[:, q:q + 1], a2[:, q, :],
                                                start=(q == 0), stop=(q == M2 - 1))
                    last.then_inc(s_yps, 1)

            def body(k, first=False, last=False):
                for g in range(NG):
                    if g + T_RING < NG:
                        interact(k, g + T_RING)
                    elif not last:
                        interact(k + 1, g + T_RING - NG)
                    reduce(k, g)
                    for step in prep_steps(k, g, first, last):
                        prep(*step)
                    if not first and g in MLP_PE:
                        mlp(k - 1, MLP_PE[g])

            pe.wait_ge(s_const, 16 * N_CONST)
            pe.wait_ge(s_ident, 1)
            for step in PROLOGUE:
                prep(*step)
            for g in range(T_RING):
                interact(0, g)
            body(0, first=True)
            with pe.Fori(1, BLOCKS - 1) as k:
                body(k)
            body(BLOCKS - 1, last=True)
            for step in MLP_PE.values():
                mlp(BLOCKS - 1, step)


def pieces_at(g):
    def needed(to):
        return PIECES if to >= NG else -(-(UNIT0[to]) // PIECE)
    return range(needed(g + LEAD) if g >= 0 else 0, needed(g + 1 + LEAD))


PROLOGUE = [(what, 0, J) for J in range(3) for what in ("round", "sub", "plain", "pairs")]


_TABLES = [f"tbl_{f}" for f in range(FIELDS)]


def kernel(**inputs):
    import numpy as np
    import concourse.bacc as bacc
    from concourse.bass_utils import run_bass_kernel_spmd

    nc = bacc.Bacc("TRN2", target_bir_lowering=False, num_devices=1)
    x = {n: np.ascontiguousarray(a) for n, a in inputs.items()}
    ids = x["ids"].reshape(BLOCKS, BT, P, CHUNKS, CF).transpose(0, 3, 2, 1, 4).reshape(BLOCKS, CHUNKS, P, BT * CF)

    pair = {}
    for i in range(FIELDS):
        for j in range(i + 1, FIELDS):
            pair[i, j] = len(pair)
    none = len(pair)
    rows = np.array([[pair.get((i, CF * J + c), none) for c in range(CF)] for i, J in UNIT_LIST])
    w_pad = np.concatenate([x["L0_rec_W"], np.zeros((1, E, E), np.float32)])
    w_stack = w_pad[rows].transpose(2, 0, 1, 3).reshape(E, NU * P)
    dw_pad = np.concatenate([x["L0_rec_dense_w"], np.zeros((1, D), np.float32)])
    dw_rows = dw_pad[rows].transpose(1, 0, 2).reshape(CF, NU * D)
    sel = np.zeros((P, D), np.float32)
    for r in range(CF):
        sel[E * r:E * r + D] = np.eye(D, dtype=np.float32)
    sel[D] = x["L0_rec_dense_b"]
    scale_shift = np.stack([np.concatenate([x["L0_rec_gamma"], np.ones(D, np.float32)]),
                            np.concatenate([x["L0_rec_beta"], np.zeros(D, np.float32)])], axis=1)
    arrays = {
        "ids_in": ids,
        **{n: x[n] for n in _TABLES},
        "ctx_in": x["dense_ctx"].reshape(BLOCKS, NB, D),
        "w_stack": w_stack, "dw_rows": dw_rows, "sel": sel, "scale_shift": scale_shift,
        "w1": x["W_top1"], "b1": x["b_top1"].reshape(M1, P).T,
        "w2": x["W_top2"].reshape(M1, P, HID2).transpose(1, 0, 2), "b2": x["b_top2"].reshape(M2, P).T,
        "w3": x["W_top3"].reshape(M2, P).T, "ident": np.eye(P, dtype=np.float32),
    }
    arrays = {n: np.ascontiguousarray(a) for n, a in arrays.items()}
    dram = {n: nc.dram_tensor(f"{n}_dram", a.shape, mybir.dt.from_np(a.dtype), kind="ExternalInput").ap()
            for n, a in arrays.items()}
    y = nc.dram_tensor("y", (BLOCKS, 1, NB), F32, kind="ExternalOutput").ap()
    dlrm_tower(nc, dram["ids_in"], [dram[n] for n in _TABLES], dram["ctx_in"], dram["w_stack"], dram["dw_rows"],
               dram["sel"], dram["scale_shift"], dram["w1"], dram["b1"], dram["w2"], dram["b2"], dram["w3"],
               dram["ident"], y)
    r = run_bass_kernel_spmd(nc, [{f"{n}_dram": a for n, a in arrays.items()}], core_ids=[0])
    return r.results[0]["y"].reshape(BATCH, 1)
```

```python
from contextlib import ExitStack

import concourse.bass as bass
from concourse import mybir

F32 = mybir.dt.float32
F32R = mybir.dt.float32r
I32 = mybir.dt.int32
ALU = mybir.AluOpType
ACT = mybir.ActivationFunctionType

P = 128
BATCH = 2048
FIELDS = 40
E = 32
D = 16
LN_EPS = 0.001
CF = P // E
CHUNKS = FIELDS // CF
NB = 256
BT = NB // P
BLOCKS = BATCH // NB
HID1, HID2 = 512, 256
M1, M2 = HID1 // P, HID2 // P

GROUPS = [(J, I) for J in range(CHUNKS) for I in range(J + 1)]
UNITS_OF = [[CF * I + r for r in range(CF if I < J else CF - 1)] for J, I in GROUPS]
GROUPS.append(GROUPS[-1])
UNITS_OF[-1:] = [UNITS_OF[-1][:2], UNITS_OF[-1][2:]]
NG = len(GROUPS)
T_RING, PROD_RING = 2, 4
assert NG % T_RING == 0 and NG % PROD_RING == 0
UNIT0 = [sum(len(u) for u in UNITS_OF[:g]) for g in range(NG)]
NU = sum(len(u) for u in UNITS_OF)
UNIT_LIST = [(i, J) for (J, _), us in zip(GROUPS, UNITS_OF) for i in us]
TILE_GROUPS = [[g for g in range(NG) if any(i % CF == tile for i in UNITS_OF[g])] for tile in range(CF)]
FIRST_G = [J * (J + 1) // 2 for J in range(CHUNKS)] + [NG]

QUARTER = 4
PIECE = CF * QUARTER
PLACES_COLS = P // 2 + CF * P
PIECES, QUARTERS = -(-NU // PIECE), -(-NU // QUARTER)
RAW_RING, HL_RING = 3, 2


def quarter_cols(q):
    return min(QUARTER, NU - q * QUARTER) * P


def piece_shape(n):
    return E * min(CF, QUARTERS - n * CF), quarter_cols(n * CF)


W_STEPS = [[("w_round", 0), ("w_sub", 0), ("w_spread", 0)]]
for _q in range(1, QUARTERS):
    _n, _what = (_q + 3) // CF, {1: "w_round", 2: "w_sub"}.get(_q % CF)
    W_STEPS.append(([(_what, _n)] if _what and _n < PIECES else []) + [("w_spread", _q)])
W_AHEAD = [sum(W_STEPS[0:5], []), sum(W_STEPS[5:11], [])]
W_AT = {}
for _q in range(11, QUARTERS):
    _J, _r = divmod(_q - 11, 6)
    W_AT.setdefault(FIRST_G[_J] + _r * (_J + 1) // 6, []).extend(W_STEPS[_q])

AHEAD = 3
STEADY = {J: (-5, -3, -3, -1) for J in range(AHEAD, CHUNKS)}
END = {J: (-2, -2, -2, -1) if J in (5, 6, 7) else STEADY[J] for J in range(AHEAD, CHUNKS)}
START = {J: (-1, -1, -1, -1) if J < 6 else STEADY[J] for J in range(AHEAD - 1, CHUNKS)}


def prep_table(own):
    table = {}
    for J in range(AHEAD):
        g = FIRST_G[CHUNKS - 1] + AHEAD * J
        for what, at in (("round", g - 1), ("sub", g + 1), ("plain", g + 2), ("pairs", g + 3)):
            table.setdefault(at, []).append((what, 1, J))
    for J, ats in own.items():
        for what, at in zip(("round", "sub", "plain", "pairs"), ats):
            table.setdefault(FIRST_G[J] + at, []).append((what, 0, J))
    return table


PREP_FIRST, PREP, PREP_LAST = prep_table(START), prep_table(STEADY), prep_table(END)
PROLOGUE = []
for _J in range(AHEAD - 1):
    PROLOGUE += [(what, 0, n) for what, n in W_AHEAD[_J]]
    PROLOGUE += [(what, 0, _J) for what in ("round", "sub", "plain", "pairs")]
COLS_SLOT = [J if J < 3 else 3 - (J + 1) % 2 for J in range(CHUNKS)]
COLS_BEFORE = [(1, 0), (1, 1), (1, CHUNKS - 2), (1, CHUNKS - 1), (0, 2)] + [(0, J - 2) for J in range(5, CHUNKS)]

MLP_PE = {8: "z", 15: "ct", 21: "h1-0", 22: "h1-1", 24: "h1-2", 26: "h1-3", 28: "h2-0", 29: "h2-1", 30: "h2-2",
          31: "h2-3", 32: "h2-4", 34: "h2-5", 36: "h2-6", 37: "h2-7", 39: "y-0", 40: "y-1"}
MLP_ACT = {10: "std", 22: "h1-0", 26: "h1-1", 37: "h2", 40: "y"}
MLP_DVE = {10: "stats", 13: "norm", 17: "cat"}


def steps_at(k, g, first, last):
    if first:
        for what, n in W_AT.get(g, ()):
            yield what, k, n
    for what, ahead, J in (PREP_FIRST if first else PREP_LAST if last else PREP).get(g, ()):
        if not (ahead and last):
            yield what, k + ahead, J


def before(step, other):
    order = PROLOGUE + [s for g in range(NG) for s in steps_at(0, g, True, False)]
    return sum(what == other for what, _, _ in order[:order.index(step)])


def dlrm_tower(nc, ids, tables, ctx_in, w_pieces, dw_rows, sel, scale_shift, w1, b1, w2, b2, w3,
               ident_in, places_in, y_out):
    with ExitStack() as stack:
        def sb(name, shape, dt=F32):
            return stack.enter_context(nc.sbuf_tensor(name, shape, dt))

        def psum(name, shape):
            return stack.enter_context(nc.psum_tensor(name, shape, F32))

        def sem(name):
            return stack.enter_context(nc.semaphore(name))

        t_ps = [psum(f"t_ps{n}", [P, CF, NB]) for n in range(T_RING)]
        h_ps = psum("h_ps", [P, 512])
        pair_ps = psum("pair_ps", [P, CF // 2, NB])
        plain_ps = psum("plain_ps", [P, 512])
        mlp_ps = psum("mlp_ps", [P, 512])

        w_raw = sb("w_raw", [P, RAW_RING, QUARTER * P])
        w_split = sb("w_split", [P, NU * P], F32R)
        dw = sb("dw", [P, NU * D])
        idx = sb("idx", [P, CHUNKS, BT * CF], I32)
        x_rows = sb("x_rows", [P, CHUNKS, BT, P])
        x_hl = sb("x_hl", [P, 2, BT * CF, 2, E], F32R)
        x_stack = sb("x_stack", [P, FIELDS, NB], F32R)
        x_cols = sb("x_cols", [P, 4, NB])
        prod = sb("prod", [P, PROD_RING, CF, NB])
        ident = sb("ident", [P, P])
        ident_r = sb("ident_r", [P, P], F32R)
        h_sb = sb("h_sb", [P, NB])
        sel_sb = sb("sel_sb", [P, D])
        stats = sb("stats", [P, BT, 6])
        mv = sb("mv", [P, BT, 2])
        var = sb("var", [P, BT])
        std = sb("std", [P, BT])
        no_use = sb("no_use", [P, 1])
        cat = sb("cat", [P, BT, 2 * D])
        ss = sb("ss", [2 * D, 2])
        cat_t = h_sb[0:2 * D, :]
        y_sb = h_sb[P // 2:P // 2 + 1, :]
        w1_sb = sb("w1_sb", [2 * D, HID1])
        b1_sb = sb("b1_sb", [P, M1])
        w2_sb = sb("w2_sb", [P, M1, HID2])
        b2_sb = sb("b2_sb", [P, M2])
        w3_sb = sb("w3_sb", [P, M2])
        spare = x_stack[:, FIELDS - 3 * CF:FIELDS, :].rearrange("p i b -> p (i b)")
        hl_cols = HL_RING * 2 * QUARTER * P
        assert hl_cols + PLACES_COLS <= 3 * CF * NB
        w_hl = spare[:, 0:hl_cols].rearrange("p (n h c) -> p n h c", n=HL_RING, h=2)
        places = spare[:, hl_cols:hl_cols + PLACES_COLS]
        places_raw = x_cols[:, :, :].rearrange("p n b -> p (n b)")[:, 0:PLACES_COLS]
        assert max(W_AT) < FIRST_G[CHUNKS - 3] + START[CHUNKS - 3][3]
        spread_ps = [mlp_ps, plain_ps]
        assert RAW_RING * QUARTER * P >= (M1 + M2) * NB
        mlp_sb = w_raw[:, :, :].rearrange("p r c -> p (r c)")
        a1 = mlp_sb[:, 0:M1 * NB].rearrange("p (m b) -> p m b", b=NB)
        a2 = mlp_sb[:, M1 * NB:(M1 + M2) * NB].rearrange("p (m b) -> p m b", b=NB)

        s_first = sem("s_first")
        s_const = sem("s_const")
        s_dw = sem("s_dw")
        s_raw = [sem(f"s_raw{n}") for n in range(RAW_RING)]
        s_whi = sem("s_whi")
        s_wlo = sem("s_wlo")
        s_spread = sem("s_spread")
        s_w = sem("s_w")
        s_idx = [sem(f"s_idx{J}") for J in range(CHUNKS)]
        s_slot = sem("s_slot")
        s_x = [sem(f"s_x{n}") for n in range(CHUNKS)]
        s_hi = sem("s_hi")
        s_hl = sem("s_hl")
        s_pair = sem("s_pair")
        s_stack = sem("s_stack")
        s_plain = sem("s_plain")
        s_cols = sem("s_cols")
        s_ident = sem("s_ident")
        s_t = sem("s_t")
        s_prod = sem("s_prod")
        s_red = sem("s_red")
        s_ones = sem("s_ones")
        s_h = sem("s_h")
        s_z = sem("s_z")
        s_st = sem("s_st")
        s_carry = sem("s_carry")
        s_var = sem("s_var")
        s_std = sem("s_std")
        s_ctx = sem("s_ctx")
        s_norm = sem("s_norm")
        s_catps = sem("s_catps")
        s_cat = sem("s_cat")
        s_h1 = sem("s_h1")
        s_a1 = sem("s_a1")
        s_h2 = sem("s_h2")
        s_a2 = sem("s_a2")
        s_yps = sem("s_yps")
        s_y = sem("s_y")
        s_out = sem("s_out")

        N_CONST = 7
        GATHERED = 16 * BT * CF

        block = stack.enter_context(nc.Block())

        @block.sync
        def _(sp):
            def load_ids(k, J):
                sp.dma_start(idx[:, J, :], ids[k, J]).then_inc(s_idx[J], 16)

            def load_ctx(k):
                sp.dma_start(cat[:, :, D:2 * D], ctx_in[k].rearrange("(t p) d -> p t d", p=P)).then_inc(s_ctx, 16)

            def store_y(k):
                sp.wait_ge(s_y, k + 1)
                sp.dma_start(y_out[k], y_sb[:, :]).then_inc(s_out, 16)

            def load_weights(n):
                rows, cols = piece_shape(n)
                if n >= RAW_RING:
                    sp.wait_ge(s_wlo, n - RAW_RING + 1)
                sp.dma_start(w_raw[0:rows, n % RAW_RING, 0:cols],
                             w_pieces[n, 0:rows, 0:cols]).then_inc(s_raw[n % RAW_RING], 16)

            load_ids(0, 0)
            load_weights(0)
            sp.dma_start(places_raw, places_in).then_inc(s_first, 16)
            sp.dma_start(ident[:, :], ident_in).then_inc(s_first, 16)
            for n in range(1, RAW_RING):
                load_weights(n)
            for J in range(1, CHUNKS):
                load_ids(0, J)
            for c in range(CF):
                sp.dma_start(dw[E * c:E * c + E, :], dw_rows[c:c + 1, :].to_broadcast([E, NU * D])).then_inc(s_dw, 16)
            for dst, src in ((sel_sb, sel), (ss, scale_shift), (w1_sb, w1), (b1_sb, b1),
                             (w2_sb, w2), (b2_sb, b2), (w3_sb, w3)):
                sp.dma_start(dst[:], src).then_inc(s_const, 16)
            load_ctx(0)

            for n in range(RAW_RING, PIECES):
                load_weights(n)
            for J in range(CHUNKS):
                sp.wait_ge(s_x[J], GATHERED)
                load_ids(1, J)

            def body(k, first=False, last=False):
                for J in range(CHUNKS):
                    if not (first or last):
                        sp.wait_ge(s_x[J], (k + 1) * GATHERED)
                        load_ids(k + 1, J)
                if not first:
                    store_y(k - 1)
                    sp.wait_ge(s_catps, k)
                    load_ctx(k)

            body(0, first=True)
            with sp.Fori(1, BLOCKS - 1) as k:
                body(k)
            body(BLOCKS - 1, last=True)
            store_y(BLOCKS - 1)
            sp.wait_ge(s_out, 16 * BLOCKS)

        @block.gpsimd
        def _(pool):
            def body(k, first=False):
                for J in range(CHUNKS):
                    pool.wait_ge(s_idx[J], (k + 1) * 16)
                    if not first:
                        pool.wait_ge(s_plain, (k - 1) * CHUNKS + (J + 1))
                    pool.sem_inc(s_slot, 1)
                    for t in range(BT):
                        for c in range(CF):
                            pool.indirect_dma_start(
                                x_rows[:, J, t, E * c:E * c + E], None, tables[CF * J + c],
                                bass.IndirectOffsetOnAxis(ap=idx[:, J, t * CF + c:t * CF + c + 1], axis=0),
                            ).then_inc(s_x[J], 16)

            body(0, first=True)
            with pool.Fori(1, BLOCKS) as k:
                body(k)

        @block.scalar
        def _(act):
            def weights(what, n):
                if what == "w_round":
                    rows, cols = piece_shape(n)
                    act.wait_ge(s_raw[n % RAW_RING], 16 * (n // RAW_RING + 1))
                    if n >= HL_RING:
                        act.wait_ge(s_spread, CF * (n - HL_RING + 1))
                    nc.scalar.activation(w_hl[0:rows, n % HL_RING, 0, 0:cols], w_raw[0:rows, n % RAW_RING, 0:cols],
                                         ACT.Copy).then_inc(s_whi, 1)
                elif what == "w_spread":
                    cols = quarter_cols(n)
                    act.wait_ge(s_spread, n + 1)
                    nc.scalar.activation(w_split[:, n * QUARTER * P:n * QUARTER * P + cols],
                                         spread_ps[n % 2][:, 0:cols], ACT.Copy).then_inc(s_w, 1)

            def prep(what, k, J):
                if what.startswith("w_"):
                    weights(what, J)
                elif what == "round":
                    act.wait_ge(s_x[J], (k + 1) * GATHERED)
                    if J >= 2 or not (isinstance(k, int) and k == 0):
                        act.wait_ge(s_pair, k * CHUNKS + (J - 1))
                    nc.scalar.activation(x_hl[:, J % 2, :, 0, :],
                                         x_rows[:, J].rearrange("p t (c e) -> p (t c) e", e=E),
                                         ACT.Copy).then_inc(s_hi, 1)
                elif what == "pairs":
                    act.wait_ge(s_pair, k * CHUNKS + (J + 1))
                    for c in range(2):
                        for half in range(2):
                            last = nc.scalar.activation(
                                x_stack[P // 2 * half:P // 2 * (half + 1), CF * J + c:CF * J + CF:2, :],
                                pair_ps[P // 2 * c:P // 2 * (c + 1), :, :], ACT.Copy)
                    last.then_inc(s_stack, 1)
                elif what == "plain":
                    act.wait_ge(s_plain, k * CHUNKS + (J + 1))
                    back, chunk = COLS_BEFORE[J]
                    if not (isinstance(k, int) and k < back):
                        act.wait_ge(s_prod, k * NG + (FIRST_G[chunk + 1] - back * NG))
                    nc.scalar.activation(x_cols[:, COLS_SLOT[J], :], plain_ps[:, 0:NB], ACT.Copy).then_inc(s_cols, 1)

            def mlp(k, step):
                if step == "std":
                    nc.scalar.activation(no_use[:, :], ident[:, 0:1], ACT.Sqrt)
                    act.wait_ge(s_var, k + 1)
                    nc.scalar.activation(std[:, :], var[:, :], ACT.Sqrt).then_inc(s_std, 1)
                elif step.startswith("h1"):
                    half = int(step[-1])
                    act.wait_ge(s_h1, k * 2 + (half + 1))
                    for m in range(2):
                        last = nc.scalar.activation(a1[:, 2 * half + m, :], mlp_ps[:, m * NB:m * NB + NB], ACT.Relu,
                                                    bias=b1_sb[:, 2 * half + m:2 * half + m + 1])
                    last.then_inc(s_a1, 1)
                elif step == "h2":
                    act.wait_ge(s_h2, k + 1)
                    for m in range(M2):
                        last = nc.scalar.activation(a2[:, m, :], mlp_ps[:, m * NB:m * NB + NB], ACT.Relu,
                                                    bias=b2_sb[:, m:m + 1])
                    last.then_inc(s_a2, 1)
                elif step == "y":
                    act.wait_ge(s_yps, k + 1)
                    if not (isinstance(k, int) and k == 0):
                        act.wait_ge(s_out, k * 16)
                    nc.scalar.activation(y_sb[:, :], mlp_ps[0:1, 0:NB], ACT.Copy).then_inc(s_y, 1)

            def save_h(k):
                act.wait_ge(s_red, (k + 1) * NG)
                if not (isinstance(k, int) and k == 0):
                    act.wait_ge(s_out, k * 16)
                nc.scalar.activation(h_sb[:, :], h_ps[:, 0:NB], ACT.Copy).then_inc(s_h, 1)

            def body(k, first=False, last=False):
                for g in range(NG):
                    for step in steps_at(k, g, first, last):
                        prep(*step)
                    if not first and g in MLP_ACT:
                        mlp(k - 1, MLP_ACT[g])
                save_h(k)

            act.wait_ge(s_first, 16 * 2)
            nc.scalar.activation(places, places_raw, ACT.Copy)
            nc.scalar.activation(ident_r[:, :], ident[:, :], ACT.Copy).then_inc(s_ident, 1)
            for step in PROLOGUE:
                prep(*step)
            body(0, first=True)
            act.wait_ge(s_const, 16 * N_CONST)
            with act.Fori(1, BLOCKS - 1) as k:
                body(k)
            body(BLOCKS - 1, last=True)
            for step in MLP_ACT.values():
                mlp(BLOCKS - 1, step)

        @block.vector
        def _(dve):
            nc.vector.memset(h_ps[:, 0:NB], 1.0).then_inc(s_ones, 1)

            def weights(what, n):
                if what == "w_sub":
                    rows, cols = piece_shape(n)
                    dve.wait_ge(s_whi, n + 1)
                    nc.vector.tensor_tensor(w_hl[0:rows, n % HL_RING, 1, 0:cols], w_raw[0:rows, n % RAW_RING, 0:cols],
                                            w_hl[0:rows, n % HL_RING, 0, 0:cols].bitcast(F32),
                                            ALU.subtract).then_inc(s_wlo, 1)

            def prep(what, k, J):
                if what.startswith("w_"):
                    weights(what, J)
                elif what == "sub":
                    dve.wait_ge(s_hi, k * CHUNKS + (J + 1))
                    nc.vector.tensor_tensor(x_hl[:, J % 2, :, 1, :],
                                            x_rows[:, J].rearrange("p t (c e) -> p (t c) e", e=E),
                                            x_hl[:, J % 2, :, 0, :].bitcast(F32), ALU.subtract).then_inc(s_hl, 1)

            def multiply(k, g):
                J, I = GROUPS[g]
                n = len(UNITS_OF[g])
                if I == 0:
                    dve.wait_ge(s_cols, k * CHUNKS + (J + 1))
                dve.wait_ge(s_t, k * NG + (g + 1))
                if g >= PROD_RING or not (isinstance(k, int) and k == 0):
                    dve.wait_ge(s_red, k * NG + (g + 1 - PROD_RING))
                xj = x_cols[:, COLS_SLOT[J], :].rearrange("p (u b) -> p u b", u=1).to_broadcast([P, n, NB])
                nc.vector.tensor_tensor(prod[:, g % PROD_RING, 0:n, :], t_ps[g % T_RING][:, 0:n, :], xj,
                                        ALU.mult).then_inc(s_prod, 1)

            def mlp(k, step):
                z = mlp_ps[:, 0:BT * D].rearrange("p (t d) -> p t d", d=D)
                if step == "stats":
                    dve.wait_ge(s_z, k + 1)
                    for t in range(BT):
                        last = nc.vector.bn_stats(stats[:, t, :], z[:, t, :])
                    last.then_inc(s_st, 1)
                    dve.wait_ge(s_st, k * 3 + 1)
                    dve.sem_inc(s_carry, 1)
                    for t in range(BT):
                        last = nc.vector.bn_aggr(mv[:, t, :], stats[:, t, :])
                    last.then_inc(s_st, 1)
                    dve.wait_ge(s_st, k * 3 + 2)
                    nc.vector.tensor_scalar(var[:, :], mv[:, :, 1], LN_EPS, None, ALU.add).then_inc(s_var, 1)
                elif step == "norm":
                    dve.wait_ge(s_std, k + 1)
                    nc.vector.reciprocal(std[:, :], std[:, :]).then_inc(s_st, 1)
                    dve.wait_ge(s_st, k * 3 + 3)
                    if not (isinstance(k, int) and k == 0):
                        dve.wait_ge(s_catps, k)
                    for t in range(BT):
                        last = nc.vector.tensor_scalar(cat[:, t, 0:D], z[:, t, :], mv[:, t, 0:1], std[:, t:t + 1],
                                                       ALU.subtract, ALU.mult)
                    last.then_inc(s_norm, 1)
                elif step == "cat":
                    dve.wait_ge(s_catps, k + 1)
                    nc.vector.tensor_scalar(cat_t[:, :], mlp_ps[0:2 * D, 0:NB], ss[:, 0:1], ss[:, 1:2],
                                            ALU.mult, ALU.add).then_inc(s_cat, 1)

            def body(k, first=False, last=False):
                for g in range(NG):
                    multiply(k, g)
                    for step in steps_at(k, g, first, last):
                        prep(*step)
                    if not first and g in MLP_DVE:
                        mlp(k - 1, MLP_DVE[g])

            for step in PROLOGUE:
                prep(*step)
            body(0, first=True)
            dve.wait_ge(s_const, 16 * N_CONST)
            with dve.Fori(1, BLOCKS - 1) as k:
                body(k)
            body(BLOCKS - 1, last=True)
            for step in MLP_DVE.values():
                mlp(BLOCKS - 1, step)

        @block.tensor
        def _(pe):
            def weights(what, n):
                if what == "w_spread":
                    piece, quarter = divmod(n, CF)
                    cols = quarter_cols(n)
                    pe.wait_ge(s_wlo, piece + 1)
                    if n >= 2:
                        pe.wait_ge(s_w, n - 1)
                    plains = before(("w_spread", 0, n), "plain")
                    if n % 2 and plains:
                        pe.wait_ge(s_cols, plains)
                    rows = piece_shape(piece)[0]
                    for lo in range(2):
                        at = P * quarter + P // 2 * (1 - lo)
                        last = nc.tensor.matmul(spread_ps[n % 2][:, 0:cols], places[0:rows, at:at + P],
                                                w_hl[0:rows, piece % HL_RING, lo, 0:cols],
                                                start=(lo == 0), stop=(lo == 1))
                    last.then_inc(s_spread, 1)

            def prep(what, k, J):
                again = not (isinstance(k, int) and k == 0)
                if what.startswith("w_"):
                    weights(what, J)
                elif what == "pairs":
                    if J or again:
                        pe.wait_ge(s_stack, k * CHUNKS + J)
                    for q in range(CF // 2):
                        for t in range(BT):
                            two = x_hl[:, J % 2, t * CF + 2 * q:t * CF + 2 * q + 2, :, :]
                            last = nc.tensor.matmul(pair_ps[:, q, t * P:t * P + P],
                                                    two.rearrange("p c h e -> p (c h e)"), ident_r[:, :],
                                                    start=True, stop=True)
                    last.then_inc(s_pair, 1)
                elif what == "plain":
                    pe.wait_ge(s_hl, k * CHUNKS + (J + 1))
                    if J or again:
                        pe.wait_ge(s_cols, k * CHUNKS + J)
                    if not again:
                        pe.wait_ge(s_w, before((what, 0, J), "w_spread"))
                    for t in range(BT):
                        last = nc.tensor.transpose(plain_ps[:, t * P:t * P + P], x_rows[:, J, t, :], ident[:, :])
                    last.then_inc(s_plain, 1)

            def interact(k, g):
                J, I = GROUPS[g]
                if I == J:
                    pe.wait_ge(s_stack, k * CHUNKS + (J + 1))
                if isinstance(k, int) and k == 0:
                    pe.wait_ge(s_w, (UNIT0[g] + len(UNITS_OF[g]) - 1) // QUARTER + 1)
                if g >= T_RING or not (isinstance(k, int) and k == 0):
                    pe.wait_ge(s_prod, k * NG + (g + 1 - T_RING))
                for r, i in enumerate(UNITS_OF[g]):
                    u = UNIT0[g] + r
                    last = nc.tensor.matmul(t_ps[g % T_RING][:, r, :], w_split[:, u * P:u * P + P], x_stack[:, i, :],
                                            start=True, stop=True)
                last.then_inc(s_t, 1)

            def reduce(k, g):
                pe.wait_ge(s_prod, k * NG + (g + 1))
                if g == 0:
                    if isinstance(k, int) and k == 0:
                        pe.wait_ge(s_dw, 16 * CF)
                        pe.wait_ge(s_ones, 1)
                    else:
                        pe.wait_ge(s_h, k)
                for r, i in enumerate(UNITS_OF[g]):
                    u, tile = UNIT0[g] + r, i % CF
                    last = nc.tensor.matmul(h_ps[E * tile:E * tile + D, 0:NB], dw[:, u * D:u * D + D],
                                            prod[:, g % PROD_RING, r, :], start=(g == TILE_GROUPS[tile][0]),
                                            stop=(g == TILE_GROUPS[tile][-1]), tile_position=(0, E * tile))
                last.then_inc(s_red, 1)

            def mlp(k, step):
                if step == "z":
                    pe.wait_ge(s_h, k + 1)
                    if not (isinstance(k, int) and k == 0):
                        pe.wait_ge(s_y, k)
                    for t in range(BT):
                        last = nc.tensor.matmul(mlp_ps[:, t * D:t * D + D], h_sb[:, t * P:t * P + P], sel_sb[:, :],
                                                start=True, stop=True)
                    last.then_inc(s_z, 1)
                elif step == "ct":
                    pe.wait_ge(s_norm, k + 1)
                    pe.wait_ge(s_ctx, k * 16 + 16)
                    for t in range(BT):
                        last = nc.tensor.transpose(mlp_ps[0:2 * D, t * P:t * P + P], cat[:, t, :], ident[:, :])
                    last.then_inc(s_catps, 1)
                elif step.startswith("h1"):
                    q = int(step[-1])
                    if q == 0:
                        pe.wait_ge(s_cat, k + 1)
                    if q == 2:
                        pe.wait_ge(s_a1, k * 2 + 1)
                    last = nc.tensor.matmul(mlp_ps[:, q % 2 * NB:q % 2 * NB + NB], w1_sb[:, q * P:q * P + P],
                                            cat_t[:, :], start=True, stop=True)
                    if q % 2:
                        last.then_inc(s_h1, 1)
                elif step.startswith("h2"):
                    m, q = divmod(int(step[-1]), M1)
                    if step == "h2-0":
                        pe.wait_ge(s_a1, k * 2 + 2)
                    last = nc.tensor.matmul(mlp_ps[:, m * NB:m * NB + NB], w2_sb[:, q, m * P:m * P + P], a1[:, q, :],
                                            start=(q == 0), stop=(q == M1 - 1))
                    if step == "h2-7":
                        last.then_inc(s_h2, 1)
                elif step.startswith("y"):
                    q = int(step[-1])
                    if q == 0:
                        pe.wait_ge(s_a2, k + 1)
                    last = nc.tensor.matmul(mlp_ps[0:1, 0:NB], w3_sb[:, q:q + 1], a2[:, q, :],
                                            start=(q == 0), stop=(q == M2 - 1))
                    if q == M2 - 1:
                        last.then_inc(s_yps, 1)

            def body(k, first=False, last=False):
                for g in range(NG):
                    if g + T_RING < NG:
                        interact(k, g + T_RING)
                    elif not last:
                        interact(k + 1, g + T_RING - NG)
                    reduce(k, g)
                    for step in steps_at(k, g, first, last):
                        prep(*step)
                    if not first and g in MLP_PE:
                        mlp(k - 1, MLP_PE[g])

            pe.wait_ge(s_first, 16 * 2)
            pe.wait_ge(s_ident, 1)
            for step in PROLOGUE:
                prep(*step)
            for g in range(T_RING):
                interact(0, g)
            body(0, first=True)
            pe.wait_ge(s_const, 16 * N_CONST)
            with pe.Fori(1, BLOCKS - 1) as k:
                body(k)
            body(BLOCKS - 1, last=True)
            for step in MLP_PE.values():
                mlp(BLOCKS - 1, step)


_TABLES = [f"tbl_{f}" for f in range(FIELDS)]


def kernel(**inputs):
    import numpy as np
    import concourse.bacc as bacc
    from concourse.bass_utils import run_bass_kernel_spmd

    nc = bacc.Bacc("TRN2", target_bir_lowering=False, num_devices=1)
    x = {n: np.ascontiguousarray(a) for n, a in inputs.items()}
    ids = x["ids"].reshape(BLOCKS, BT, P, CHUNKS, CF).transpose(0, 3, 2, 1, 4).reshape(BLOCKS, CHUNKS, P, BT * CF)

    pair = {}
    for i in range(FIELDS):
        for j in range(i + 1, FIELDS):
            pair[i, j] = len(pair)
    none = len(pair)
    rows = np.array([[pair.get((i, CF * J + c), none) for c in range(CF)] for i, J in UNIT_LIST])
    w_pad = np.concatenate([x["L0_rec_W"], np.zeros((1, E, E), np.float32)])
    w_units = np.zeros((PIECES * PIECE, E, P), np.float32)
    w_units[:NU] = w_pad[rows].transpose(0, 2, 1, 3).reshape(NU, E, P)
    w_pieces = w_units.reshape(PIECES, CF, QUARTER, E, P).transpose(0, 1, 3, 2, 4).reshape(PIECES, P, QUARTER * P)
    dw_pad = np.concatenate([x["L0_rec_dense_w"], np.zeros((1, D), np.float32)])
    dw_rows = dw_pad[rows].transpose(1, 0, 2).reshape(CF, NU * D)
    sel = np.zeros((P, D), np.float32)
    for r in range(CF):
        sel[E * r:E * r + D] = np.eye(D, dtype=np.float32)
    sel[D] = x["L0_rec_dense_b"]
    places = np.zeros((P, PLACES_COLS), np.float32)
    for q in range(CF):
        for at in (P * q + P // 2, P * q + P // 2 + E):
            places[E * q:E * q + E, at:at + E] = np.eye(E, dtype=np.float32)
    scale_shift = np.stack([np.concatenate([x["L0_rec_gamma"], np.ones(D, np.float32)]),
                            np.concatenate([x["L0_rec_beta"], np.zeros(D, np.float32)])], axis=1)
    arrays = {
        "ids_in": ids,
        **{n: x[n] for n in _TABLES},
        "ctx_in": x["dense_ctx"].reshape(BLOCKS, NB, D),
        "w_pieces": w_pieces, "dw_rows": dw_rows, "sel": sel, "scale_shift": scale_shift,
        "w1": x["W_top1"], "b1": x["b_top1"].reshape(M1, P).T,
        "w2": x["W_top2"].reshape(M1, P, HID2).transpose(1, 0, 2), "b2": x["b_top2"].reshape(M2, P).T,
        "w3": x["W_top3"].reshape(M2, P).T, "ident": np.eye(P, dtype=np.float32), "places": places,
    }
    arrays = {n: np.ascontiguousarray(a) for n, a in arrays.items()}
    dram = {n: nc.dram_tensor(f"{n}_dram", a.shape, mybir.dt.from_np(a.dtype), kind="ExternalInput").ap()
            for n, a in arrays.items()}
    y = nc.dram_tensor("y", (BLOCKS, 1, NB), F32, kind="ExternalOutput").ap()
    dlrm_tower(nc, dram["ids_in"], [dram[n] for n in _TABLES], dram["ctx_in"], dram["w_pieces"], dram["dw_rows"],
               dram["sel"], dram["scale_shift"], dram["w1"], dram["b1"], dram["w2"], dram["b2"], dram["w3"],
               dram["ident"], dram["places"], y)
    r = run_bass_kernel_spmd(nc, [{f"{n}_dram": a for n, a in arrays.items()}], core_ids=[0])
    return r.results[0]["y"].reshape(BATCH, 1)
```
